# Optimizing a Trainium2 kernel written in Bass

```python
import numpy as np
import jax
import jax.numpy as jnp

def _softmax(x, axis=-1):
    return jax.nn.softmax(x, axis=axis)

def _gelu(x):
    return jax.nn.gelu(x, approximate=True)

def _silu(x):
    return jax.nn.silu(x)

def _sigmoid(x):
    return jax.nn.sigmoid(x)

def _layernorm(x, axis=-1, eps=1e-05):
    m = jnp.mean(x, axis=axis, keepdims=True)
    v = jnp.var(x, axis=axis, keepdims=True)
    return (x - m) / jnp.sqrt(v + eps)

def _scatter_add(tgt, idx, src, axis=0):
    return tgt.at[idx].add(src)

def _segment_sum(src, seg, n):
    return jax.ops.segment_sum(src, seg, n)
kernel_name = 'mk_xattn_ffn_d1_seqx_r8_addac0'

def setup_inputs(seed: int=0):
    np.random.seed(seed)
    _w = jnp.asarray

    def _rec_inputs():
        import jax
        import jax.numpy as jnp
        _rk = jax.random.key(seed)
        x = -0.0002928 + 1 * jax.random.normal(jax.random.fold_in(_rk, 1), (16, 256, 128), jnp.float32)
        _lenS = 256 - jax.random.randint(jax.random.fold_in(_rk, 7), (16,), 0, max(1, 256 // 4) + 1, jnp.int32)
        _lenS2 = 64 - jax.random.randint(jax.random.fold_in(_rk, 8), (16,), 0, max(1, 64 // 4) + 1, jnp.int32)
        _ctx_1024P = jax.random.normal(jax.random.fold_in(_rk, 11), (16, 16, 128), jnp.float32)
        _ctx_1024c = jax.random.dirichlet(jax.random.fold_in(_rk, 511), 0.3 * jnp.ones((16,), jnp.float32), (16, 64))
        _ctx_1024t = jnp.einsum('bsk,bkd->bsd', _ctx_1024c, _ctx_1024P)
        _ctx_1024t = _ctx_1024t * jax.lax.rsqrt(jnp.mean(jnp.square(_ctx_1024t)) + 1e-12) * 0.953939
        ctx_1024 = -1.39393e-06 + 0.999914 * (_ctx_1024t + 0.3 * jax.random.normal(jax.random.fold_in(_rk, 611), (16, 64, 128), jnp.float32))
        return (x, ctx_1024)
    x, ctx_1024 = _rec_inputs()

    def _L0_xattn_setup():
        import jax, jax.numpy as jnp
        import numpy as np
        EMBED_DIM = 128
        NUM_HEADS = 16
        HEAD_DIM = EMBED_DIM // NUM_HEADS
        B, NQ, K = (2, 256, 256)
        key = jax.random.key(seed)
        ks = jax.random.split(key, 11)
        s = 1.0 / np.sqrt(EMBED_DIM)
        return {'Q_input': jax.random.normal(ks[0], (B, NQ, EMBED_DIM), jnp.float32), 'K_input': jax.random.normal(ks[1], (B, K, EMBED_DIM), jnp.float32), 'V_input': jax.random.normal(ks[2], (B, K, EMBED_DIM), jnp.float32), 'Wq': jax.random.normal(ks[3], (EMBED_DIM, EMBED_DIM), jnp.float32) * s, 'bq': jnp.zeros((EMBED_DIM,), jnp.float32), 'Wk': jax.random.normal(ks[4], (EMBED_DIM, EMBED_DIM), jnp.float32) * s, 'bk': jnp.zeros((EMBED_DIM,), jnp.float32), 'Wv': jax.random.normal(ks[5], (EMBED_DIM, EMBED_DIM), jnp.float32) * s, 'bv': jnp.zeros((EMBED_DIM,), jnp.float32), 'Wo': jax.random.normal(ks[6], (EMBED_DIM, EMBED_DIM), jnp.float32) * s, 'bo': jnp.zeros((EMBED_DIM,), jnp.float32)}
    _L0_xattn_all = _L0_xattn_setup()
    _L0_xattn_in = {k: v for k, v in _L0_xattn_all.items() if k in ('Wq', 'bq', 'Wk', 'bk', 'Wv', 'bv', 'Wo', 'bo')}
    del _L0_xattn_all

    def _L0_ffn_setup():
        import jax, jax.numpy as jnp
        import numpy as np
        D_MODEL = 128
        D_FF = 512
        NUM_EXPERTS = 8
        B, N = (16, 128)
        key = jax.random.key(seed)
        ks = jax.random.split(key, 7)
        s_in = 1.0 / np.sqrt(D_MODEL)
        s_ff = 1.0 / np.sqrt(D_FF)
        return {'x': jax.random.normal(ks[0], (B, N, D_MODEL), dtype=jnp.float32), 'Wr': jax.random.uniform(ks[1], (D_MODEL, NUM_EXPERTS), jnp.float32, -s_in, s_in), 'br': jax.random.uniform(ks[2], (NUM_EXPERTS,), jnp.float32, -s_in, s_in), 'W1': jax.random.uniform(ks[3], (NUM_EXPERTS, D_MODEL, D_FF), jnp.float32, -s_in, s_in), 'b1': jax.random.uniform(ks[4], (NUM_EXPERTS, D_FF), jnp.float32, -s_in, s_in), 'W2': jax.random.uniform(ks[5], (NUM_EXPERTS, D_FF, D_MODEL), jnp.float32, -s_ff, s_ff), 'b2': jax.random.uniform(ks[6], (NUM_EXPERTS, D_MODEL), jnp.float32, -s_ff, s_ff)}
    _L0_ffn_all = _L0_ffn_setup()
    _L0_ffn_in = {k: v for k, v in _L0_ffn_all.items() if k in ('Wr', 'br', 'W1', 'b1', 'W2', 'b2')}
    del _L0_ffn_all
    return {'x': x, 'ctx_1024': ctx_1024, 'L0_xattn_Wq': _L0_xattn_in['Wq'], 'L0_xattn_bq': _L0_xattn_in['bq'], 'L0_xattn_Wk': _L0_xattn_in['Wk'], 'L0_xattn_bk': _L0_xattn_in['bk'], 'L0_xattn_Wv': _L0_xattn_in['Wv'], 'L0_xattn_bv': _L0_xattn_in['bv'], 'L0_xattn_Wo': _L0_xattn_in['Wo'], 'L0_xattn_bo': _L0_xattn_in['bo'], 'L0_ffn_Wr': _L0_ffn_in['Wr'], 'L0_ffn_br': _L0_ffn_in['br'], 'L0_ffn_W1': _L0_ffn_in['W1'], 'L0_ffn_b1': _L0_ffn_in['b1'], 'L0_ffn_W2': _L0_ffn_in['W2'], 'L0_ffn_b2': _L0_ffn_in['b2']}

def reference(x, ctx_1024, L0_xattn_Wq, L0_xattn_bq, L0_xattn_Wk, L0_xattn_bk, L0_xattn_Wv, L0_xattn_bv, L0_xattn_Wo, L0_xattn_bo, L0_ffn_Wr, L0_ffn_br, L0_ffn_W1, L0_ffn_b1, L0_ffn_W2, L0_ffn_b2):
    import jax
    import jax.numpy as jnp

    def _L0_xattn_ref(Q_input, K_input, V_input, Wq, bq, Wk, bk, Wv, bv, Wo, bo):
        import jax, jax.numpy as jnp
        import numpy as np
        EMBED_DIM = 128
        NUM_HEADS = 16
        HEAD_DIM = EMBED_DIM // NUM_HEADS
        B, NQ, K = (2, 256, 256)
        b, n_q, _ = Q_input.shape
        k = K_input.shape[1]
        Q = Q_input @ Wq.T + bq
        Kp = K_input @ Wk.T + bk
        V = V_input @ Wv.T + bv
        Q = Q.reshape(b, n_q, NUM_HEADS, HEAD_DIM).transpose(0, 2, 1, 3)
        Kp = Kp.reshape(b, k, NUM_HEADS, HEAD_DIM).transpose(0, 2, 1, 3)
        V = V.reshape(b, k, NUM_HEADS, HEAD_DIM).transpose(0, 2, 1, 3)
        scores = jnp.einsum('bhqd,bhkd->bhqk', Q, Kp) / jnp.sqrt(jnp.float32(HEAD_DIM))
        weights = jax.nn.softmax(scores, axis=-1)
        attn = jnp.einsum('bhqk,bhkd->bhqd', weights, V)
        attn = attn.transpose(0, 2, 1, 3).reshape(b, n_q, EMBED_DIM)
        return attn @ Wo.T + bo

    def _L0_ffn_ref(x, Wr, br, W1, b1, W2, b2):
        import jax, jax.numpy as jnp
        import numpy as np
        D_MODEL = 128
        D_FF = 512
        NUM_EXPERTS = 8
        B, N = (16, 128)
        scores = jnp.einsum('bh,he->be', x.mean(axis=1), Wr) + br
        top1 = jnp.argmax(scores, axis=-1)
        w1 = W1[top1]
        c1 = b1[top1]
        w2 = W2[top1]
        c2 = b2[top1]
        h = jax.nn.relu(jnp.einsum('bnh,bhf->bnf', x, w1) + c1[:, None, :])
        out = jnp.einsum('bnf,bfh->bnh', h, w2) + c2[:, None, :]
        return out
    x = x + _L0_xattn_ref(_layernorm(x, axis=-1), ctx_1024, ctx_1024, L0_xattn_Wq, L0_xattn_bq, L0_xattn_Wk, L0_xattn_bk, L0_xattn_Wv, L0_xattn_bv, L0_xattn_Wo, L0_xattn_bo)
    x = x + _L0_ffn_ref(_layernorm(x, axis=-1), L0_ffn_Wr, L0_ffn_br, L0_ffn_W1, L0_ffn_b1, L0_ffn_W2, L0_ffn_b2)
    return x

_drawn_inputs = setup_inputs


def setup_inputs(seed=0):
    import zlib

    import numpy as np

    out = dict(_drawn_inputs(seed))
    spreads = {'L0_xattn_bq': (0.0, 0.1),
     'L0_xattn_bk': (0.0, 0.8),
     'L0_xattn_bv': (0.0, 0.1),
     'L0_xattn_bo': (0.0, 0.1)}
    factors = {'L0_ffn_b1': 3.152}
    for name, (base, spread) in spreads.items():
        noise = np.random.default_rng([zlib.crc32(name.encode()), seed]).standard_normal(out[name].shape)
        drawn = base * np.exp(spread * noise) if base else spread * noise
        out[name] = jnp.asarray(drawn.astype(out[name].dtype))
    for name, factor in factors.items():
        out[name] = (out[name] * factor).astype(out[name].dtype)
    return out
```

```python
import numpy as np

import concourse.bass as bass
from concourse import mybir
from contextlib import ExitStack

F32 = mybir.dt.float32
F32R = mybir.dt.float32r
U32 = mybir.dt.uint32
ALU = mybir.AluOpType
ACT = mybir.ActivationFunctionType
AX_X = mybir.AxisListType.X

P = 128
HEADS = 16
HG = 4
GROUPS = HEADS // HG
PARTS = 3
EPS = 1e-5

_WIDTHS = [("ident", P), ("wq_t", P), ("wk_t", P), ("wv_t", P), ("wo_t", P), ("bv_row", P), ("bo_row", P),
           ("wr", 8), ("br_row", 8), ("bq_col", 1), ("bk_col", 1), ("k_mask", HG), ("v_mask", 64), ("head_sel", HEADS)]
COL = {}
_at = 0
for _name, _w in _WIDTHS:
    COL[_name] = (_at, _at + _w)
    _at += _w
CONST_W = _at


def xattn_moe_kernel(nc, x, ctx_t, consts, experts, out):
    B, TOK, D = x.shape
    KEYS = ctx_t.shape[2] // 2
    QT = TOK // P
    HD = D // HEADS
    FC = 4
    F = FC * P
    NE = experts.shape[0]
    GR = HG * HD
    SR = PARTS * GR
    MR = SR + HEADS
    GK = HG * KEYS
    PAIRS = HEADS // 2
    SCALE = 1.0 / float(np.sqrt(np.float32(HD)))
    assert D == P and QT == 2 and 2 * KEYS == P and SR == 96

    with ExitStack() as ctx:
        def sb(name, shape, dt=F32):
            return ctx.enter_context(nc.sbuf_tensor(name, shape, dt))

        def psum(name, shape):
            return ctx.enter_context(nc.psum_tensor(name, shape, F32))

        def sem(name):
            return ctx.enter_context(nc.semaphore(name))

        cst = sb("cst", [P, CONST_W])
        ctx_sb = sb("ctx_sb", [P, B, 2 * KEYS])
        x_sb = sb("x_sb", [P, B, QT, D])
        minus_half = sb("minus_half", [P, QT])
        eps_sb = sb("eps_sb", [P, QT])
        stats1 = sb("stats1", [P, 2, QT, 6])
        mv1 = sb("mv1", [P, 2, QT, 2])
        rstd1 = sb("rstd1", [P, 2, QT, 1])
        ve1 = sb("ve1", [P, 2, QT, 1])
        stats2 = sb("stats2", [P, 2, QT, 6])
        mv2 = sb("mv2", [P, 2, QT, 2])
        rstd2 = sb("rstd2", [P, 2, QT, 1])
        ve2 = sb("ve2", [P, 2, QT, 1])
        xn1 = sb("xn1", [P, 2, QT, D])
        xn1_t = sb("xn1_t", [P, TOK])
        q_parts = sb("q_parts", [P, 2, PARTS, TOK], F32R)
        q_stack = sb("q_stack", [P, 2, GROUPS, TOK], F32R)
        k_parts = sb("k_parts", [P, PARTS, B * KEYS], F32R)
        k_stack = sb("k_stack", [SR, GROUPS, B * KEYS])
        k_diag = sb("k_diag", [P, 2, GROUPS * GK], F32R)
        v_sb = sb("v_sb", [P, B, D])
        v_diag = sb("v_diag", [P, PAIRS, 32])
        negmax = sb("negmax", [P, 2, QT, HEADS])
        negmax_t = sb("negmax_t", [HEADS, 2, TOK], F32R)
        probs_t = sb("probs_t", [P, PAIRS, TOK])
        inv_sum = sb("inv_sum", [P, TOK])
        attn_t = sb("attn_t", [P, TOK])
        x_bo = sb("x_bo", [P, 2, QT, D])
        x1 = sb("x1", [P, 2, QT, D])
        x1_b2 = sb("x1_b2", [P, 2, QT, D])
        xn2 = sb("xn2", [P, 2, QT, D])
        xn2_t = sb("xn2_t", [P, 2, TOK])
        tok_sum = sb("tok_sum", [P, 2])
        route = sb("route", [1, NE])
        route_top = sb("route_top", [1, 8])
        expert_id = sb("expert_id", [1, 2, 8], U32)
        EW = F + FC + F + D
        ew = sb("ew", [P, 2, EW])
        hid_t = sb("hid_t", [P, FC, TOK])
        y_sb = sb("y_sb", [P, 2, QT, D])

        ps_max = [psum(f"ps_max{k}", [P, 512]) for k in range(2)]
        ps_pv = psum("ps_pv", [P, 2, TOK])
        ps_q = psum("ps_q", [P, 2, TOK])
        ps_o = psum("ps_o", [P, 2, TOK])
        ps_ring = [psum(f"ps_ring{k}", [P, 2, TOK]) for k in range(3)]

        def const(name):
            a, b = COL[name]
            return cst[:, a:b]

        def w1_of(par, c):
            return ew[:, par, c * P:(c + 1) * P]

        def b1_of(par, c):
            return ew[:, par, F + c:F + c + 1]

        def w2_of(par, c):
            return ew[:, par, F + FC + c * D:F + FC + (c + 1) * D]

        def b2_of(par):
            return ew[:, par, F + FC + F:EW]

        XLOADS = [0, 1, 4, 10, B]
        x_in = [sem(f"x_in{k}") for k in range(len(XLOADS) - 1)]
        cst_in = sem("cst_in")
        ctx_in = sem("ctx_in")
        kstack_in = sem("kstack_in")
        qstack_in = [sem(f"qstack_in{k}") for k in range(2)]
        max_in = [sem(f"max_in{k}") for k in range(2)]
        expert_in = [sem(f"expert_in{k}") for k in range(2)]
        y_out = [sem(f"y_out{k}") for k in range(2)]
        passed = [sem("sp_passed"), sem("dve_passed")]
        sel_done = sem("sel_done")
        khi_copied = sem("khi_copied")
        v_ready = sem("v_ready")
        st1_raw = sem("st1_raw")
        st1_done = sem("st1_done")
        xn1_done = sem("xn1_done")
        max_done = sem("max_done")
        qhi_copied = sem("qhi_copied")
        q_done = sem("q_done")
        vdiag_done = sem("vdiag_done")
        inv_done = sem("inv_done")
        attn_done = sem("attn_done")
        x1_done = sem("x1_done")
        st2_raw = sem("st2_raw")
        st2_done = sem("st2_done")
        xn2_done = sem("xn2_done")
        route_done = sem("route_done")
        top_done = sem("top_done")
        id_done = sem("id_done")
        y_done = sem("y_done")
        khi_done = sem("khi_done")
        xn1t_done = sem("xn1t_done")
        qhi_done = sem("qhi_done")
        maxt_done = sem("maxt_done")
        hid_done = sem("hid_done")
        exp_done = sem("exp_done")
        xn2t_done = sem("xn2t_done")
        k_proj = sem("k_proj")
        v_proj = sem("v_proj")
        tr1_done = sem("tr1_done")
        q_proj = sem("q_proj")
        smax_done = sem("smax_done")
        tmax_done = sem("tmax_done")
        s_done = sem("s_done")
        pv_done = sem("pv_done")
        o_proj = sem("o_proj")
        tr2_done = sem("tr2_done")
        logit_done = sem("logit_done")
        up_done = sem("up_done")
        down_done = sem("down_done")
        half_set = sem("half_set")
        ve1_done = sem("ve1_done")
        rstd1_done = sem("rstd1_done")
        xbo_done = sem("xbo_done")
        kdiag_done = sem("kdiag_done")
        x1b2_done = sem("x1b2_done")
        ve2_done = sem("ve2_done")
        rstd2_done = sem("rstd2_done")

        LAST = B + 3

        def hold(engine, i):
            if not isinstance(i, int):
                engine.sem_inc(passed[engine is nc.vector], 1)

        def pipeline(engine, step, after_step=None):
            def peeled(t):
                step(0, t, lambda k: 0 <= t + k < B, lambda k: t + k)
                if after_step and t in after_step:
                    after_step[t]()
            for t in range(-1, 5):
                peeled(t)
            with engine.Fori(2, B // 2 - 1) as i:
                for j in (1, 2):
                    step(i, j, lambda k: True, lambda k: 4)
            for t in range(B - 1, LAST):
                peeled(t)

        block = ctx.enter_context(nc.Block())

        @block.sync
        def _(sp):
            def load_x(k):
                a, b = XLOADS[k], XLOADS[k + 1]
                sp.dma_start(x_sb[:, a:b], x[a:b].rearrange("b (p q) d -> p b q d", q=QT)).then_inc(x_in[k], 16)

            load_x(0)
            load_x(1)
            load_x(2)
            load_x(3)

            sp.wait_ge(khi_done, 2)
            sp.wait_ge(khi_copied, 4)
            for g in range(GROUPS):
                sp.dma_start(k_stack[:, g, :], k_parts[GR * g:GR * (g + 1)].bitcast(F32)).then_inc(kstack_in, 16)

            def step(i, j, has, age):
                if has(0):
                    n, u, par = 2 * i + j, i + j // 2, j % 2
                    sp.wait_ge(q_done, n + 1)
                    hold(sp, i)
                    if age(0) >= 2:
                        sp.wait_ge(s_done, GROUPS * (n - 1))
                    for g in range(GROUPS):
                        sp.dma_start(q_stack[0:SR, par, g, :].bitcast(F32),
                                     q_parts[GR * g:GR * (g + 1), par].bitcast(F32)).then_inc(qstack_in[par], 16)
                if has(-1):
                    n, par = 2 * i + j - 1, (j - 1) % 2
                    sp.wait_ge(maxt_done, n + 1)
                    sp.dma_start(q_stack[SR:MR, par].bitcast(F32),
                                 negmax_t[:, par, :].bitcast(F32).unsqueeze(1).to_broadcast([HEADS, GROUPS, TOK])
                                 ).then_inc(max_in[par], 16)
                if has(-2):
                    n, par = 2 * i + j - 2, (j - 2) % 2
                    if age(-2) >= 2:
                        sp.wait_ge(down_done, n - 1)
                        sp.wait_ge(x1b2_done, n - 1)
                    sp.wait_ge(id_done, n + 1)
                    hold(sp, i)
                    e = sp.value_load(expert_id[0:1, par, 0:1], min_val=0, max_val=NE - 1)
                    sp.dma_start(ew[:, par, :], experts[bass.ds(e, 1)].rearrange("o p c -> p (o c)")
                                 ).then_inc(expert_in[par], 16)
                if has(-3):
                    n, par = 2 * i + j - 3, (j - 3) % 2
                    sp.wait_ge(y_done, n + 1)
                    sp.dma_start(out[bass.ds(n, 1)].rearrange("b (p q) d -> p (b q d)", q=QT),
                                 y_sb[:, par].rearrange("p q d -> p (q d)")).then_inc(y_out[par], 16)

            pipeline(sp, step)
            for par in range(2):
                sp.wait_ge(y_out[par], 16 * (B // 2))

        @block.gpsimd
        def _(pool):
            nc.gpsimd.memset(minus_half[:], -0.5).then_inc(half_set, 1)
            nc.gpsimd.memset(eps_sb[:], EPS).then_inc(half_set, 1)

            def rsqrt(i, j, mv, ve, rstd, st_done, ve_done, rstd_done):
                n, par = 2 * i + j, j % 2
                pool.wait_ge(st_done, n + 1)
                nc.gpsimd.tensor_tensor(ve[:, par], mv[:, par, :, 1:2], eps_sb[:].unsqueeze(2), ALU.add
                                        ).then_inc(ve_done, 1)
                pool.wait_ge(ve_done, n + 1)
                nc.gpsimd.tensor_tensor(rstd[:, par], ve[:, par], minus_half[:].unsqueeze(2), ALU.pow
                                        ).then_inc(rstd_done, 1)

            def step(i, j, has, age):
                if has(1):
                    rsqrt(i, j + 1, mv1, ve1, rstd1, st1_done, ve1_done, rstd1_done)
                if has(-2):
                    n, par = 2 * i + j - 2, (j - 2) % 2
                    if age(-2) >= 2:
                        pool.wait_ge(x1_done, n - 1)
                    nc.gpsimd.tensor_tensor(x_bo[:, par], x_sb[:, bass.ds(n, 1)].rearrange("p o q d -> p (o q) d"),
                                            const("bo_row").unsqueeze(1).to_broadcast([P, QT, D]), ALU.add
                                            ).then_inc(xbo_done, 1)
                if has(0):
                    n, par = 2 * i + j, j % 2
                    if age(0) >= 2:
                        pool.wait_ge(s_done, GROUPS * (n - 1))
                    for g in range(GROUPS):
                        nc.gpsimd.tensor_tensor(
                            k_diag[0:SR, par, g * GK:(g + 1) * GK].rearrange("r (h k) -> r h k", h=HG),
                            k_stack[:, g, bass.ds(n * KEYS, KEYS)].unsqueeze(1).to_broadcast([SR, HG, KEYS]),
                            const("k_mask")[0:SR].unsqueeze(2).to_broadcast([SR, HG, KEYS]), ALU.mult
                        ).then_inc(kdiag_done, 1)
                if has(-3):
                    n, u, par = 2 * i + j - 3, i + (j - 3) // 2, (j - 3) % 2
                    pool.wait_ge(expert_in[par], 16 * (u + 1))
                    if age(-3) >= 2:
                        pool.wait_ge(y_done, n - 1)
                    nc.gpsimd.tensor_tensor(x1_b2[:, par], x1[:, par],
                                            b2_of(par).unsqueeze(1).to_broadcast([P, QT, D]), ALU.add
                                            ).then_inc(x1b2_done, 1)
                if has(-2):
                    rsqrt(i, j - 2, mv2, ve2, rstd2, st2_done, ve2_done, rstd2_done)

            pool.wait_ge(half_set, 2)
            pool.wait_ge(x_in[0], 16)
            def rest_loaded():
                pool.wait_ge(cst_in, 16)
                pool.wait_ge(kstack_in, 16 * GROUPS)
                for k in range(1, len(x_in)):
                    pool.wait_ge(x_in[k], 16)
            pipeline(pool, step, {-1: rest_loaded})

        @block.scalar
        def _(act):
            act.dma_start(cst[:], consts).then_inc(cst_in, 16)
            act.dma_start(ctx_sb[:], ctx_t.rearrange("b p k -> p b k")).then_inc(ctx_in, 16)
            act.wait_ge(cst_in, 16)
            for c in range(2):
                act.wait_ge(k_proj, c + 1)
                nc.scalar.activation(k_parts[:, 0, c * 512:(c + 1) * 512], ps_max[c][:], ACT.Identity,
                                     bias=const("bk_col")).then_inc(khi_done, 1)

            def exp_group(i, j, g):
                n = 2 * i + j
                act.wait_ge(s_done, GROUPS * n + g + 1)
                nc.scalar.activation(probs_t[:, 2 * g:2 * g + 2, :], ps_ring[(2 + g) % 3][:], ACT.Exp,
                                     scale=SCALE).then_inc(exp_done, 1)

            def step(i, j, has, age):
                if has(0):
                    n, u, par = 2 * i + j, i + j // 2, j % 2
                    act.wait_ge(q_proj, n + 1)
                    if age(0) >= 2:
                        act.wait_ge(qstack_in[par], 16 * GROUPS * u)
                    nc.scalar.activation(q_parts[:, par, 0, :], ps_q[:, 1, :], ACT.Identity,
                                         bias=const("bq_col")).then_inc(qhi_done, 1)
                if has(-1):
                    n, u, par = 2 * i + j - 1, i + (j - 1) // 2, (j - 1) % 2
                    act.wait_ge(tmax_done, n + 1)
                    if age(-1) >= 2:
                        act.wait_ge(max_in[par], 16 * u)
                    nc.scalar.copy(negmax_t[:, par, :], ps_q[0:HEADS, 1, :]).then_inc(maxt_done, 1)
                if has(-3):
                    n, u, par = 2 * i + j - 3, i + (j - 3) // 2, (j - 3) % 2
                    act.wait_ge(expert_in[par], 16 * (u + 1))
                    if age(-3) >= 1:
                        act.wait_ge(down_done, n)
                    for c in range(FC):
                        act.wait_ge(up_done, 2 * n + c // 2 + 1)
                        nc.scalar.activation(hid_t[:, c, :], ps_ring[c // 2][:, c % 2, :], ACT.Relu,
                                             bias=b1_of(par, c)).then_inc(hid_done, 1)
                if has(1):
                    n = 2 * i + j + 1
                    act.wait_ge(tr1_done, n + 1)
                    if age(1) >= 1:
                        act.wait_ge(q_proj, n)
                    nc.scalar.copy(xn1_t[:], ps_q[:, 0, :]).then_inc(xn1t_done, 1)
                if has(-1):
                    if age(-1) >= 1:
                        act.wait_ge(pv_done, 2 * i + j - 1)
                    exp_group(i, j - 1, 0)
                    exp_group(i, j - 1, 1)
                if has(-2):
                    n, par = 2 * i + j - 2, (j - 2) % 2
                    act.wait_ge(tr2_done, n + 1)
                    if age(-2) >= 2:
                        act.wait_ge(up_done, 2 * (n - 1))
                        act.wait_ge(logit_done, n - 1)
                    nc.scalar.activation(xn2_t[:, par, :], ps_o[:, 1, :], ACT.Identity,
                                         accum_out=tok_sum[:, par:par + 1]).then_inc(xn2t_done, 1)
                if has(-1):
                    exp_group(i, j - 1, 2)
                    exp_group(i, j - 1, 3)

            pipeline(act, step)

        @block.tensor
        def _(pe):
            ident = const("ident")
            pe.wait_ge(cst_in, 16)
            pe.wait_ge(ctx_in, 16)
            for c in range(2):
                nc.tensor.matmul(ps_max[c][:], const("wk_t"), ctx_sb[:, c * (B // 2):(c + 1) * (B // 2), 0:KEYS],
                                 start=True, stop=True).then_inc(k_proj, 1)

            def project_v():
                for n in range(B):
                    bank = ([ps_o] + ps_ring)[n // 4].rearrange("p a t -> p (a t)")
                    mm = nc.tensor.matmul(bank[:, (n % 4) * D:(n % 4 + 1) * D],
                                          ctx_sb[:, n, :], const("wv_t"), start=True, stop=True)
                    if n % 4 == 3:
                        mm.then_inc(v_proj, 1)
                pe.wait_ge(v_ready, 4)

            def scores_for_max(i, j, q, age):
                n, par = 2 * i + j, j % 2
                for half in range(2):
                    use = 2 * q + half
                    if age >= 1 or use >= 2:
                        pe.wait_ge(max_done, 4 * n + use - 1)
                    for g in (2 * half, 2 * half + 1):
                        mm = nc.tensor.matmul(ps_max[half][:, (g % 2) * GK:(g % 2 + 1) * GK],
                                              q_stack[0:SR, par, g, q * P:(q + 1) * P],
                                              k_diag[0:SR, par, g * GK:(g + 1) * GK], start=True, stop=True)
                    mm.then_inc(smax_done, 1)

            def scores_t(i, j, g, age, ffn_before):
                n, par = 2 * i + j, j % 2
                if g == 0 and age >= 1:
                    pe.wait_ge(exp_done, 4 * n)
                if g in (1, 2):
                    if age >= 1:
                        pe.wait_ge(exp_done, 4 * (n - 1) + g + 1)
                    if ffn_before:
                        pe.wait_ge(hid_done, 4 * (n - 2) + 2 * g)
                if g == 3:
                    pe.wait_ge(exp_done, 4 * n + 1)
                for c in range(2):
                    mm = nc.tensor.matmul(ps_ring[(2 + g) % 3][:, c, :],
                                          k_diag[0:MR, par, (2 * g + c) * P:(2 * g + c + 1) * P],
                                          q_stack[0:MR, par, g, :], start=True, stop=True)
                mm.then_inc(s_done, 1)

            def up(i, j, half, ring_used):
                n, par = 2 * i + j, j % 2
                if ring_used:
                    pe.wait_ge(exp_done, 4 * (n + 1) + half + 2)
                for c in (2 * half, 2 * half + 1):
                    mm = nc.tensor.matmul(ps_ring[half][:, c % 2, :], w1_of(par, c), xn2_t[:, par, :],
                                          start=True, stop=True)
                mm.then_inc(up_done, 1)

            def down(i, j, half):
                n, par = 2 * i + j, j % 2
                for c in (2 * half, 2 * half + 1):
                    pe.wait_ge(hid_done, 4 * n + c + 1)
                    for q in range(QT):
                        mm = nc.tensor.matmul(ps_pv[:, 0, q * P:(q + 1) * P], hid_t[:, c, q * P:(q + 1) * P],
                                              w2_of(par, c), start=(c == 0 and q == 0), stop=(c == FC - 1),
                                              skip_group_check=True)
                if half == 1:
                    mm.then_inc(down_done, 1)

            def step(i, j, has, age):
                if has(-1):
                    n, u, par = 2 * i + j - 1, i + (j - 1) // 2, (j - 1) % 2
                    pe.wait_ge(qstack_in[par], 16 * GROUPS * (u + 1))
                    pe.wait_ge(kdiag_done, GROUPS * (n + 1))
                    scores_for_max(i, j - 1, 0, age(-1))
                if has(0):
                    n = 2 * i + j
                    pe.wait_ge(xn1t_done, n + 1)
                    nc.tensor.matmul(ps_q[:, 1, :], const("wq_t"), xn1_t[:], start=True, stop=True
                                     ).then_inc(q_proj, 1)
                if has(-1):
                    scores_for_max(i, j - 1, 1, age(-1))
                if has(-2):
                    n = 2 * i + j - 2
                    if has(-3):
                        pe.wait_ge(attn_done, n)
                    if has(-4):
                        pe.wait_ge(y_done, n - 1)
                    pe.wait_ge(vdiag_done, n + 1)
                    for a in range(2):
                        pe.wait_ge(exp_done, GROUPS * n + 2 * a + 2)
                        for part in range(2):
                            for tile in range(4):
                                c = 4 * a + tile
                                m0, m1 = COL["v_mask"][0] + 32 * a, COL["v_mask"][0] + 32 * (a + 1)
                                weights = v_diag[:, c, :] if part == 0 else cst[:, m0:m1]
                                mm = nc.tensor.matmul(ps_pv[32 * tile:32 * (tile + 1), part, :], weights,
                                                      probs_t[:, c, :], start=(a == 0 and part == 0),
                                                      stop=(a == 1), tile_position=(0, 32 * tile),
                                                      skip_group_check=True)
                    mm.then_inc(pv_done, 1)
                if has(-1):
                    n, par = 2 * i + j - 1, (j - 1) % 2
                    pe.wait_ge(max_done, 4 * (n + 1))
                    if has(0):
                        pe.wait_ge(q_done, n + 2)
                    elif age(-1) >= 1:
                        pe.wait_ge(maxt_done, n)
                    for q in range(QT):
                        mm = nc.tensor.transpose(ps_q[0:HEADS, 1, q * P:(q + 1) * P], negmax[:, par, q, :], ident)
                    mm.then_inc(tmax_done, 1)
                if has(-3):
                    n, u, par = 2 * i + j - 3, i + (j - 3) // 2, (j - 3) % 2
                    pe.wait_ge(expert_in[par], 16 * (u + 1))
                    pe.wait_ge(xn2t_done, n + 1)
                    up(i, j - 3, 0, has(-2))
                if has(-2):
                    n = 2 * i + j - 2
                    pe.wait_ge(attn_done, n + 1)
                    if age(-2) >= 1:
                        pe.wait_ge(route_done, n)
                    for q in range(QT):
                        mm = nc.tensor.matmul(ps_o[:, 0, q * P:(q + 1) * P], attn_t[:, q * P:(q + 1) * P],
                                              const("wo_t"), start=True, stop=True)
                    mm.then_inc(o_proj, 1)
                if has(-3):
                    up(i, j - 3, 1, has(-2))
                if has(1):
                    n, par = 2 * i + j + 1, (j + 1) % 2
                    pe.wait_ge(xn1_done, QT * (n + 1))
                    if has(-1):
                        pe.wait_ge(maxt_done, n - 1)
                    elif has(0):
                        pe.wait_ge(q_done, n)
                    for q in range(QT):
                        mm = nc.tensor.transpose(ps_q[:, 0, q * P:(q + 1) * P], xn1[:, par, q, :], ident)
                    mm.then_inc(tr1_done, 1)
                if has(-3):
                    n = 2 * i + j - 3
                    if has(-2):
                        pe.wait_ge(attn_done, n + 2)
                    elif age(-3) >= 1:
                        pe.wait_ge(y_done, n)
                    down(i, j - 3, 0)
                if has(-1):
                    n, u, par = 2 * i + j - 1, i + (j - 1) // 2, (j - 1) % 2
                    pe.wait_ge(max_in[par], 16 * (u + 1))
                    scores_t(i, j - 1, 0, age(-1), has(-3))
                    scores_t(i, j - 1, 1, age(-1), has(-3))
                if has(-2):
                    n, par = 2 * i + j - 2, (j - 2) % 2
                    pe.wait_ge(xn2_done, QT * (n + 1))
                    for q in range(QT):
                        mm = nc.tensor.transpose(ps_o[:, 1, q * P:(q + 1) * P], xn2[:, par, q, :], ident)
                    mm.then_inc(tr2_done, 1)
                if has(-1):
                    scores_t(i, j - 1, 2, age(-1), has(-3))
                    scores_t(i, j - 1, 3, age(-1), has(-3))
                if has(-2):
                    n, par = 2 * i + j - 2, (j - 2) % 2
                    pe.wait_ge(xn2t_done, n + 1)
                    nc.tensor.matmul(ps_o[0:1, 0, 0:NE], tok_sum[:, par:par + 1], const("wr"),
                                     start=True, stop=True).then_inc(logit_done, 1)
                if has(-3):
                    down(i, j - 3, 1)

            pipeline(pe, step, {0: project_v})

        @block.vector
        def _(dve):
            dve.wait_ge(x_in[0], 16)
            dve.wait_ge(cst_in, 16)

            def prepare_k():
                a, b = COL["head_sel"]
                for par in range(2):
                    nc.vector.tensor_copy(
                        k_diag[SR:MR, par, :].rearrange("r (h k) -> r h k", h=HEADS),
                        cst[SR:MR, a:b].unsqueeze(2).to_broadcast([HEADS, HEADS, KEYS])).then_inc(sel_done, 1)
                for c in range(2):
                    cols = slice(c * 512, (c + 1) * 512)
                    dve.wait_ge(khi_done, c + 1)
                    nc.vector.scalar_tensor_tensor(
                        out=k_parts[:, 2, cols], in0=ps_max[c][:], scalar=const("bk_col"),
                        in1=k_parts[:, 0, cols].bitcast(F32), op0=ALU.add, op1=ALU.subtract).then_inc(khi_copied, 1)
                    nc.vector.tensor_copy(k_parts[:, 1, cols], k_parts[:, 0, cols].bitcast(F32)
                                          ).then_inc(khi_copied, 1)
                for k in range(1, len(x_in)):
                    dve.wait_ge(x_in[k], 16)

            def prepare_v():
                for c in range(4):
                    dve.wait_ge(v_proj, c + 1)
                    bank = ([ps_o] + ps_ring)[c]
                    nc.vector.tensor_tensor(v_sb[:, 4 * c:4 * (c + 1), :],
                                            bank.rearrange("p a (b d) -> p (a b) d", d=D),
                                            const("bv_row").unsqueeze(1).to_broadcast([P, 4, D]), ALU.add
                                            ).then_inc(v_ready, 1)
                dve.wait_ge(v_ready, 4)

            def spread_v(i, j, age):
                n = 2 * i + j
                if age >= 1:
                    dve.wait_ge(pv_done, n)
                nc.vector.tensor_tensor(
                    v_diag[:].rearrange("p (a t) c -> p a t c", a=2),
                    v_sb[:, bass.ds(n, 1), :].rearrange("p o (t c) -> p o t c", c=32).to_broadcast([P, 2, 4, 32]),
                    const("v_mask").rearrange("p (a c) -> p a c", a=2).unsqueeze(2).to_broadcast([P, 2, 4, 32]),
                    ALU.mult).then_inc(vdiag_done, 1)

            def reduce_max(i, j, q, half):
                n, par = 2 * i + j, j % 2
                dve.wait_ge(smax_done, 4 * n + 2 * q + half + 1)
                nc.vector.tensor_reduce(negmax[:, par, q, half * 8:(half + 1) * 8],
                                        ps_max[half][:].rearrange("p (h k) -> p h k", k=KEYS),
                                        AX_X, ALU.max, negate=True).then_inc(max_done, 1)

            def step(i, j, has, age):
                if has(1):
                    n, par = 2 * i + j + 1, (j + 1) % 2
                    for q in range(QT):
                        st = nc.vector.bn_stats(stats1[:, par, q, :],
                                                x_sb[:, bass.ds(n, 1), q, :].rearrange("p o d -> p (o d)"))
                    st.then_inc(st1_raw, 1)
                if has(-1):
                    if age(-1) >= 2:
                        dve.wait_ge(tmax_done, 2 * i + j - 2)
                    reduce_max(i, j - 1, 0, 0)
                if has(1):
                    dve.wait_ge(st1_raw, n + 1)
                    if age(1) >= 2:
                        dve.wait_ge(xn1_done, QT * (n - 1))
                if has(-1):
                    reduce_max(i, j - 1, 0, 1)
                if has(1):
                    for q in range(QT):
                        st = nc.vector.bn_aggr(mv1[:, par, q, :], stats1[:, par, q, :])
                    st.then_inc(st1_done, 1)
                if has(0):
                    n0, par0 = 2 * i + j, j % 2
                    dve.wait_ge(qhi_done, n0 + 1)
                    nc.vector.scalar_tensor_tensor(
                        out=q_parts[:, par0, 1, :], in0=ps_q[:, 1, :], scalar=const("bq_col"),
                        in1=q_parts[:, par0, 0, :].bitcast(F32), op0=ALU.add, op1=ALU.subtract
                    ).then_inc(qhi_copied, 1)
                    nc.vector.tensor_copy(q_parts[:, par0, 2, :], q_parts[:, par0, 0, :].bitcast(F32)
                                          ).then_inc(q_done, 1)
                if has(-1):
                    reduce_max(i, j - 1, 1, 0)
                    reduce_max(i, j - 1, 1, 1)
                if has(1):
                    dve.wait_ge(rstd1_done, n + 1)
                    if age(1) >= 2:
                        dve.wait_ge(tr1_done, n - 1)
                    for q in range(QT):
                        nc.vector.tensor_scalar(xn1[:, par, q, :],
                                                x_sb[:, bass.ds(n, 1), q, :].rearrange("p o d -> p (o d)"),
                                                mv1[:, par, q, 0:1], rstd1[:, par, q, :],
                                                ALU.subtract, ALU.mult).then_inc(xn1_done, 1)
                if has(-2):
                    n, par = 2 * i + j - 2, (j - 2) % 2
                    dve.wait_ge(pv_done, n + 1)
                    if age(-2) >= 1:
                        dve.wait_ge(attn_done, n)
                        dve.wait_ge(o_proj, n)
                    nc.vector.reciprocal(inv_sum[:], ps_pv[:, 1, :]).then_inc(inv_done, 1)
                    dve.wait_ge(inv_done, n + 1)
                    nc.vector.tensor_tensor(attn_t[:], ps_pv[:, 0, :], inv_sum[:], ALU.mult).then_inc(attn_done, 1)
                if has(-2):
                    n, par = 2 * i + j - 2, (j - 2) % 2
                    dve.wait_ge(o_proj, n + 1)
                    dve.wait_ge(xbo_done, n + 1)
                    if age(-2) >= 2:
                        dve.wait_ge(x1b2_done, n - 1)
                        dve.wait_ge(xn2_done, QT * (n - 1))
                    nc.vector.tensor_tensor(x1[:, par], ps_o[:, 0, :].rearrange("p (q d) -> p q d", q=QT),
                                            x_bo[:, par], ALU.add).then_inc(x1_done, 1)
                    dve.wait_ge(x1_done, n + 1)
                    for q in range(QT):
                        st = nc.vector.bn_stats(stats2[:, par, q, :], x1[:, par, q, :])
                    st.then_inc(st2_raw, 1)
                    dve.wait_ge(st2_raw, n + 1)
                if has(-1):
                    spread_v(i, j - 1, age(-1))
                if has(-2):
                    for q in range(QT):
                        st = nc.vector.bn_aggr(mv2[:, par, q, :], stats2[:, par, q, :])
                    st.then_inc(st2_done, 1)
                    dve.wait_ge(rstd2_done, n + 1)
                    if age(-2) >= 2:
                        dve.wait_ge(tr2_done, n - 1)
                    for q in range(QT):
                        nc.vector.tensor_scalar(xn2[:, par, q, :], x1[:, par, q, :], mv2[:, par, q, 0:1],
                                                rstd2[:, par, q, :], ALU.subtract, ALU.mult).then_inc(xn2_done, 1)
                if has(-2):
                    n, u, par = 2 * i + j - 2, i + (j - 2) // 2, (j - 2) % 2
                    dve.wait_ge(logit_done, n + 1)
                    if age(-2) >= 1:
                        dve.wait_ge(id_done, n)
                    if age(-2) >= 2:
                        dve.wait_ge(expert_in[par], 16 * u)
                    nc.vector.scalar_tensor_tensor(out=route[:], in0=ps_o[0:1, 0, 0:NE], scalar=1.0 / TOK,
                                                   in1=const("br_row")[0:1], op0=ALU.mult, op1=ALU.add
                                                   ).then_inc(route_done, 1)
                    dve.wait_ge(route_done, n + 1)
                    hold(dve, i)
                    nc.vector.max(route_top[:], route[:]).then_inc(top_done, 1)
                    dve.wait_ge(top_done, n + 1)
                    hold(dve, i)
                    nc.vector.max_index(expert_id[:, par, :], route_top[:], route[:]).then_inc(id_done, 1)
                if has(-3):
                    n, u, par = 2 * i + j - 3, i + (j - 3) // 2, (j - 3) % 2
                    dve.wait_ge(down_done, n + 1)
                    dve.wait_ge(x1b2_done, n + 1)
                    if age(-3) >= 2:
                        dve.wait_ge(y_out[par], 16 * u)
                    nc.vector.tensor_tensor(y_sb[:, par], ps_pv[:, 0, :].rearrange("p (q d) -> p q d", q=QT),
                                            x1_b2[:, par], ALU.add).then_inc(y_done, 1)

            pipeline(dve, step, {-1: prepare_k, 0: prepare_v})


_ARGS = ["x", "ctx_t", "consts", "experts"]


def kernel(**inputs):
    import concourse.bacc as _bacc
    from concourse.bass_utils import run_bass_kernel_spmd as _run

    a = {k: np.asarray(v) for k, v in inputs.items()}
    x, ctx = a["x"], a["ctx_1024"]
    B, TOK, D = x.shape
    KEYS = ctx.shape[1]
    W1, W2 = a["L0_ffn_W1"], a["L0_ffn_W2"]
    NE, _, F = W1.shape
    HD = D // HEADS
    f32 = np.float32

    order = np.arange(D).reshape(2, 4, 2, HD).transpose(1, 0, 2, 3).reshape(D)
    parts = {name: np.zeros((P, b - a_), f32) for name, (a_, b) in COL.items()}
    parts["ident"][:] = np.eye(P, dtype=f32)
    parts["wq_t"][:] = a["L0_xattn_Wq"].T
    parts["wk_t"][:] = a["L0_xattn_Wk"].T
    parts["wv_t"][:] = a["L0_xattn_Wv"].T[:, order]
    parts["wo_t"][:] = a["L0_xattn_Wo"].T[order]
    parts["bv_row"][:] = a["L0_xattn_bv"][order][None]
    parts["bo_row"][:] = a["L0_xattn_bo"][None]
    parts["wr"][:] = a["L0_ffn_Wr"]
    parts["br_row"][:] = a["L0_ffn_br"][None]
    parts["bq_col"][:, 0] = a["L0_xattn_bq"]
    parts["bk_col"][:, 0] = a["L0_xattn_bk"]
    rows = np.arange(PARTS * HG * HD)
    parts["k_mask"][rows, rows // (PARTS * HD)] = 1.0
    col = np.arange(64)
    parts["v_mask"][:] = ((col % 32) // 8)[None] == (2 * (col // 32))[None] + (np.arange(P) // KEYS)[:, None]
    parts["head_sel"][rows.size:rows.size + HEADS] = np.eye(HEADS, dtype=f32)
    consts = np.concatenate([parts[name] for name in COL], axis=1)
    experts = np.concatenate([
        W1,
        a["L0_ffn_b1"].reshape(NE, F // P, P).transpose(0, 2, 1),
        W2.reshape(NE, F // P, P, D).transpose(0, 2, 1, 3).reshape(NE, P, F // P * D),
        np.broadcast_to(a["L0_ffn_b2"][:, None, :], (NE, P, D)),
    ], axis=2)
    arrays = {"x": x, "ctx_t": np.concatenate([ctx, ctx], axis=1).transpose(0, 2, 1), "consts": consts, "experts": experts}

    nc = _bacc.Bacc("TRN2", target_bir_lowering=False, num_devices=1)
    in_map, args = {}, []
    for name in _ARGS:
        v = np.ascontiguousarray(arrays[name])
        in_map[f"in_{name}"] = v
        args.append(nc.dram_tensor(f"in_{name}", v.shape, mybir.dt.from_np(v.dtype), kind="ExternalInput").ap())
    args.append(nc.dram_tensor("out_y", x.shape, F32, kind="ExternalOutput").ap())
    xattn_moe_kernel(nc, *args)
    r = _run(nc, [in_map], core_ids=[0])
    return r.results[0]["out_y"]
```

```python
import numpy as np

import concourse.bass as bass
from concourse import mybir
from contextlib import ExitStack

F32 = mybir.dt.float32
F32R = mybir.dt.float32r
U32 = mybir.dt.uint32
ALU = mybir.AluOpType
ACT = mybir.ActivationFunctionType
AX_X = mybir.AxisListType.X

P = 128
HEADS = 16
HG = 4
GROUPS = HEADS // HG
PARTS = 3
EPS = 1e-5

_WIDTHS = [("ident", P), ("wq_t", P), ("wk_t", P), ("wv_t", P), ("wo_t", P), ("bv_row", P), ("bo_row", P),
           ("wr", 8), ("br_row", 8), ("bq_col", 1), ("bk_col", 1), ("k_mask", HG), ("v_mask", 64), ("head_sel", HEADS)]
COL = {}
_at = 0
for _name, _w in _WIDTHS:
    COL[_name] = (_at, _at + _w)
    _at += _w
CONST_W = _at


def xattn_moe_kernel(nc, x, ctx_t, consts, experts, out):
    B, TOK, D = x.shape
    KEYS = ctx_t.shape[2] // 2
    QT = TOK // P
    HD = D // HEADS
    FC = 4
    F = FC * P
    NE = experts.shape[0]
    GR = HG * HD
    SR = PARTS * GR
    MR = SR + HEADS
    GK = HG * KEYS
    PAIRS = HEADS // 2
    SCALE = 1.0 / float(np.sqrt(np.float32(HD)))
    assert D == P and QT == 2 and 2 * KEYS == P and SR == 96

    with ExitStack() as ctx:
        def sb(name, shape, dt=F32):
            return ctx.enter_context(nc.sbuf_tensor(name, shape, dt))

        def psum(name, shape):
            return ctx.enter_context(nc.psum_tensor(name, shape, F32))

        def sem(name):
            return ctx.enter_context(nc.semaphore(name))

        cst = sb("cst", [P, CONST_W])
        ctx_sb = sb("ctx_sb", [P, B, 2 * KEYS])
        x_sb = sb("x_sb", [P, B, QT, D])
        minus_half = sb("minus_half", [P, QT])
        minus_one = sb("minus_one", [P, QT])
        eps_sb = sb("eps_sb", [P, QT])
        stats1 = sb("stats1", [P, 2, QT, 6])
        mv1 = sb("mv1", [P, 2, QT, 2])
        rstd1 = sb("rstd1", [P, 2, QT, 1])
        ve1 = sb("ve1", [P, 2, QT, 1])
        nm1 = sb("nm1", [P, 2, QT, 1])
        shift1 = sb("shift1", [P, 2, QT, 1])
        stats2 = sb("stats2", [P, 2, QT, 6])
        mv2 = sb("mv2", [P, 2, QT, 2])
        rstd2 = sb("rstd2", [P, 2, QT, 1])
        ve2 = sb("ve2", [P, 2, QT, 1])
        xn1 = sb("xn1", [P, 2, QT, D])
        xn1_t = sb("xn1_t", [P, TOK])
        q_parts = sb("q_parts", [P, 2, PARTS, TOK], F32R)
        q_stack = sb("q_stack", [P, 2, GROUPS, TOK], F32R)
        k_parts = sb("k_parts", [P, PARTS, B * KEYS], F32R)
        k_stack = sb("k_stack", [SR, GROUPS, B * KEYS])
        k_diag = sb("k_diag", [P, 2, GROUPS * GK], F32R)
        v_sb = sb("v_sb", [P, B, D])
        v_diag = sb("v_diag", [P, 2, PAIRS, 32])
        negmax = sb("negmax", [P, 2, QT, HEADS])
        negmax_t = sb("negmax_t", [HEADS, 2, TOK], F32R)
        probs_t = sb("probs_t", [P, PAIRS, TOK])
        inv_sum = sb("inv_sum", [P, TOK])
        attn_t = sb("attn_t", [P, TOK])
        x_bo = sb("x_bo", [P, 2, QT, D])
        x1 = sb("x1", [P, 2, QT, D])
        x1_b2 = sb("x1_b2", [P, QT, D])
        xn2 = sb("xn2", [P, 2, QT, D])
        xn2_t = sb("xn2_t", [P, 2, TOK])
        tok_sum = sb("tok_sum", [P, 2])
        route = sb("route", [1, NE])
        route_top = sb("route_top", [1, 8])
        expert_id = sb("expert_id", [1, 2, 8], U32)
        EW = F + FC + F + D
        ew = sb("ew", [P, 2, EW])
        hid_t = sb("hid_t", [P, FC, TOK])
        y_sb = sb("y_sb", [P, 2, QT, D])

        ps_max = [psum(f"ps_max{k}", [P, 512]) for k in range(2)]
        ps_pv = psum("ps_pv", [P, 2, TOK])
        ps_q = psum("ps_q", [P, 2, TOK])
        ps_o = psum("ps_o", [P, 2, TOK])
        ps_ring = [psum(f"ps_ring{k}", [P, 2, TOK]) for k in range(3)]

        def const(name):
            a, b = COL[name]
            return cst[:, a:b]

        def w1_of(par, c):
            return ew[:, par, c * P:(c + 1) * P]

        def b1_of(par, c):
            return ew[:, par, F + c:F + c + 1]

        def w2_of(par, c):
            return ew[:, par, F + FC + c * D:F + FC + (c + 1) * D]

        def b2_of(par):
            return ew[:, par, F + FC + F:EW]

        XLOADS = [0, 1, 4, 10, B]
        x_in = [sem(f"x_in{k}") for k in range(len(XLOADS) - 1)]
        cst_in = sem("cst_in")
        ctx_in = sem("ctx_in")
        kstack_in = sem("kstack_in")
        qstack_in = [sem(f"qstack_in{k}") for k in range(2)]
        max_in = [sem(f"max_in{k}") for k in range(2)]
        up_in = [sem(f"up_in{k}") for k in range(2)]
        down_in = [sem(f"down_in{k}") for k in range(2)]
        y_out = [sem(f"y_out{k}") for k in range(2)]
        passed = [sem("sp_passed"), sem("dve_passed")]
        sel_done = sem("sel_done")
        khi_copied = sem("khi_copied")
        v_ready = sem("v_ready")
        st1_raw = sem("st1_raw")
        st1_done = sem("st1_done")
        max_done = sem("max_done")
        q_done = sem("q_done")
        inv_done = sem("inv_done")
        attn_done = sem("attn_done")
        x1_done = sem("x1_done")
        st2_raw = sem("st2_raw")
        st2_done = sem("st2_done")
        xn2_done = sem("xn2_done")
        route_done = sem("route_done")
        top_done = sem("top_done")
        id_done = sem("id_done")
        y_done = sem("y_done")
        khi_done = sem("khi_done")
        xn1_done = sem("xn1_done")
        xn1t_done = sem("xn1t_done")
        qhi_done = sem("qhi_done")
        qhi_copied = sem("qhi_copied")
        maxt_done = sem("maxt_done")
        hid_done = sem("hid_done")
        exp_done = sem("exp_done")
        xn2t_done = sem("xn2t_done")
        k_proj = sem("k_proj")
        v_proj = sem("v_proj")
        tr1_done = sem("tr1_done")
        q_proj = sem("q_proj")
        smax_done = sem("smax_done")
        tmax_done = sem("tmax_done")
        s_done = sem("s_done")
        sum_done = sem("sum_done")
        pv_done = sem("pv_done")
        o_proj = sem("o_proj")
        tr2_done = sem("tr2_done")
        logit_done = sem("logit_done")
        up_done = sem("up_done")
        down_done = sem("down_done")
        half_set = sem("half_set")
        ve1_done = sem("ve1_done")
        nm1_done = sem("nm1_done")
        rstd1_done = sem("rstd1_done")
        shift1_done = sem("shift1_done")
        vdiag_done = sem("vdiag_done")
        xbo_done = sem("xbo_done")
        kdiag_done = sem("kdiag_done")
        x1b2_done = sem("x1b2_done")
        ve2_done = sem("ve2_done")
        rstd2_done = sem("rstd2_done")

        LAST = B + 4

        def hold(engine, i):
            if not isinstance(i, int):
                engine.sem_inc(passed[engine is nc.vector], 1)

        def pipeline(engine, step, after_step=None):
            def peeled(t):
                step(0, t, lambda k: 0 <= t + k < B, lambda k: t + k)
                if after_step and t in after_step:
                    after_step[t]()
            for t in range(-2, 5):
                peeled(t)
            with engine.Fori(2, B // 2 - 2) as i:
                for j in (1, 2):
                    step(i, j, lambda k: True, lambda k: 4)
            for t in range(B - 3, LAST):
                peeled(t)

        block = ctx.enter_context(nc.Block())

        @block.sync
        def _(sp):
            def load_x(k):
                a, b = XLOADS[k], XLOADS[k + 1]
                sp.dma_start(x_sb[:, a:b], x[a:b].rearrange("b (p q) d -> p b q d", q=QT)).then_inc(x_in[k], 16)

            load_x(0)
            load_x(1)
            load_x(2)
            load_x(3)

            sp.wait_ge(khi_done, 2)
            sp.wait_ge(khi_copied, 4)
            for g in range(GROUPS):
                sp.dma_start(k_stack[:, g, :], k_parts[GR * g:GR * (g + 1)].bitcast(F32)).then_inc(kstack_in, 16)

            def step(i, j, has, age):
                if has(1):
                    n, u, par = 2 * i + j + 1, i + (j + 1) // 2, (j + 1) % 2
                    sp.wait_ge(q_done, n + 1)
                    sp.wait_ge(qhi_copied, n + 1)
                    hold(sp, i)
                    if age(1) >= 2:
                        sp.wait_ge(s_done, GROUPS * (n - 1))
                    for g in range(GROUPS):
                        sp.dma_start(q_stack[0:SR, par, g, :].bitcast(F32),
                                     q_parts[GR * g:GR * (g + 1), par].bitcast(F32)).then_inc(qstack_in[par], 16)
                if has(-4):
                    n, par = 2 * i + j - 4, (j - 4) % 2
                    sp.wait_ge(y_done, n + 1)
                    sp.dma_start(out[bass.ds(n, 1)].rearrange("b (p q) d -> p (b q d)", q=QT),
                                 y_sb[:, par].rearrange("p q d -> p (q d)")).then_inc(y_out[par], 16)
                if has(0):
                    n, par = 2 * i + j, j % 2
                    sp.wait_ge(maxt_done, n + 1)
                    sp.dma_start(q_stack[SR:MR, par].bitcast(F32),
                                 negmax_t[:, par, :].bitcast(F32).unsqueeze(1).to_broadcast([HEADS, GROUPS, TOK])
                                 ).then_inc(max_in[par], 16)
                if has(-2):
                    n, par = 2 * i + j - 2, (j - 2) % 2
                    sp.wait_ge(id_done, n + 1)
                    hold(sp, i)
                    if age(-2) >= 2:
                        sp.wait_ge(down_done, n - 1)
                        sp.wait_ge(x1b2_done, n - 1)
                        hold(sp, i)
                    e = sp.value_load(expert_id[0:1, par, 0:1], min_val=0, max_val=NE - 1)
                    for a, b, landed in ((0, F + FC, up_in), (F + FC, EW, down_in)):
                        sp.dma_start(ew[:, par, a:b], experts[bass.ds(e, 1), :, a:b].rearrange("o p c -> p (o c)")
                                     ).then_inc(landed[par], 16)

            pipeline(sp, step)
            for par in range(2):
                sp.wait_ge(y_out[par], 16 * (B // 2))

        @block.gpsimd
        def _(pool):
            nc.gpsimd.memset(minus_half[:], -0.5).then_inc(half_set, 1)
            nc.gpsimd.memset(eps_sb[:], EPS).then_inc(half_set, 1)
            nc.gpsimd.memset(minus_one[:], -1.0).then_inc(half_set, 1)

            def rsqrt(n, par, mv, ve, rstd, st_done, ve_done, rstd_done):
                pool.wait_ge(st_done, n + 1)
                nc.gpsimd.tensor_tensor(ve[:, par], mv[:, par, :, 1:2], eps_sb[:].unsqueeze(2), ALU.add
                                        ).then_inc(ve_done, 1)
                pool.wait_ge(ve_done, n + 1)
                nc.gpsimd.tensor_tensor(rstd[:, par], ve[:, par], minus_half[:].unsqueeze(2), ALU.pow
                                        ).then_inc(rstd_done, 1)

            def step(i, j, has, age):
                if has(-2):
                    rsqrt(2 * i + j - 2, (j - 2) % 2, mv2, ve2, rstd2, st2_done, ve2_done, rstd2_done)
                if has(-1):
                    n, par = 2 * i + j - 1, (j - 1) % 2
                    pool.wait_ge(v_ready, 4)
                    if age(-1) >= 2:
                        pool.wait_ge(pv_done, n - 1)
                    nc.gpsimd.tensor_tensor(
                        v_diag[:, par].rearrange("p (a t) c -> p a t c", a=2),
                        v_sb[:, bass.ds(n, 1), :].rearrange("p o (t c) -> p o t c", c=32).to_broadcast([P, 2, 4, 32]),
                        const("v_mask").rearrange("p (a c) -> p a c", a=2).unsqueeze(2).to_broadcast([P, 2, 4, 32]),
                        ALU.mult).then_inc(vdiag_done, 1)
                    if age(-1) >= 2:
                        pool.wait_ge(x1_done, n - 1)
                    nc.gpsimd.tensor_tensor(x_bo[:, par], x_sb[:, bass.ds(n, 1)].rearrange("p o q d -> p (o q) d"),
                                            const("bo_row").unsqueeze(1).to_broadcast([P, QT, D]), ALU.add
                                            ).then_inc(xbo_done, 1)
                if has(2):
                    n, par = 2 * i + j + 2, j % 2
                    if age(2) >= 2:
                        pool.wait_ge(xn1_done, QT * (n - 1))
                    rsqrt(n, par, mv1, ve1, rstd1, st1_done, ve1_done, rstd1_done)
                    nc.gpsimd.tensor_tensor(nm1[:, par], mv1[:, par, :, 0:1], minus_one[:].unsqueeze(2), ALU.mult
                                            ).then_inc(nm1_done, 1)
                    pool.wait_ge(rstd1_done, n + 1)
                    pool.wait_ge(nm1_done, n + 1)
                    nc.gpsimd.tensor_tensor(shift1[:, par], nm1[:, par], rstd1[:, par], ALU.mult
                                            ).then_inc(shift1_done, 1)
                if has(-3):
                    n, u, par = 2 * i + j - 3, i + (j - 3) // 2, (j - 3) % 2
                    pool.wait_ge(down_in[par], 16 * (u + 1))
                    if age(-3) >= 1:
                        pool.wait_ge(y_done, n)
                    nc.gpsimd.tensor_tensor(x1_b2[:], x1[:, par],
                                            b2_of(par).unsqueeze(1).to_broadcast([P, QT, D]), ALU.add
                                            ).then_inc(x1b2_done, 1)
                if has(1):
                    n, par = 2 * i + j + 1, (j + 1) % 2
                    if age(1) >= 2:
                        pool.wait_ge(s_done, GROUPS * (n - 1))
                    for g in range(GROUPS):
                        nc.gpsimd.tensor_tensor(
                            k_diag[0:SR, par, g * GK:(g + 1) * GK].rearrange("r (h k) -> r h k", h=HG),
                            k_stack[:, g, bass.ds(n * KEYS, KEYS)].unsqueeze(1).to_broadcast([SR, HG, KEYS]),
                            const("k_mask")[0:SR].unsqueeze(2).to_broadcast([SR, HG, KEYS]), ALU.mult
                        ).then_inc(kdiag_done, 1)

            pool.wait_ge(half_set, 3)
            pool.wait_ge(x_in[0], 16)
            def rest_loaded():
                pool.wait_ge(cst_in, 16)
                pool.wait_ge(kstack_in, 16 * GROUPS)
                for k in range(1, len(x_in)):
                    pool.wait_ge(x_in[k], 16)
            pipeline(pool, step, {-2: rest_loaded})

        @block.scalar
        def _(act):
            act.dma_start(cst[:], consts).then_inc(cst_in, 16)
            act.dma_start(ctx_sb[:], ctx_t.rearrange("b p k -> p b k")).then_inc(ctx_in, 16)
            act.wait_ge(cst_in, 16)
            for c in range(2):
                act.wait_ge(k_proj, c + 1)
                nc.scalar.activation(k_parts[:, 0, c * 512:(c + 1) * 512], ps_max[c][:], ACT.Identity,
                                     bias=const("bk_col")).then_inc(khi_done, 1)

            def exp_group(i, j, g):
                n = 2 * i + j
                act.wait_ge(s_done, GROUPS * n + g + 1)
                nc.scalar.activation(probs_t[:, 2 * g:2 * g + 2, :], ps_ring[(2 + g) % 3][:], ACT.Exp,
                                     scale=SCALE).then_inc(exp_done, 1)

            def relu(i, j, half):
                n, par = 2 * i + j, j % 2
                for c in (2 * half, 2 * half + 1):
                    act.wait_ge(up_done, 2 * n + half + 1)
                    nc.scalar.activation(hid_t[:, c, :], ps_ring[half][:, c % 2, :], ACT.Relu,
                                         bias=b1_of(par, c)).then_inc(hid_done, 1)

            def step(i, j, has, age):
                if has(1):
                    n = 2 * i + j + 1
                    act.wait_ge(tr1_done, n + 1)
                    if age(1) >= 1:
                        act.wait_ge(q_proj, n)
                    nc.scalar.copy(xn1_t[:], ps_q[:, 0, :]).then_inc(xn1t_done, 1)
                if has(-1):
                    if age(-1) >= 1:
                        act.wait_ge(pv_done, 2 * i + j - 1)
                    exp_group(i, j - 1, 0)
                if has(1):
                    n, u, par = 2 * i + j + 1, i + (j + 1) // 2, (j + 1) % 2
                    act.wait_ge(q_proj, n + 1)
                    if age(1) >= 2:
                        act.wait_ge(qstack_in[par], 16 * GROUPS * u)
                    nc.scalar.activation(q_parts[:, par, 0, :], ps_q[:, 1, :], ACT.Identity,
                                         bias=const("bq_col")).then_inc(qhi_done, 1)
                    act.wait_ge(qhi_done, n + 1)
                    nc.scalar.copy(q_parts[:, par, 2, :], q_parts[:, par, 0, :].bitcast(F32)).then_inc(qhi_copied, 1)
                if has(-1):
                    for g in range(1, GROUPS):
                        exp_group(i, j - 1, g)
                if has(-2):
                    n, par = 2 * i + j - 2, (j - 2) % 2
                    act.wait_ge(tr2_done, n + 1)
                    if age(-2) >= 2:
                        act.wait_ge(up_done, 2 * (n - 1))
                        act.wait_ge(logit_done, n - 1)
                    nc.scalar.activation(xn2_t[:, par, :], ps_o[:, 1, :], ACT.Identity,
                                         accum_out=tok_sum[:, par:par + 1]).then_inc(xn2t_done, 1)
                if has(-3):
                    n, u, par = 2 * i + j - 3, i + (j - 3) // 2, (j - 3) % 2
                    act.wait_ge(up_in[par], 16 * (u + 1))
                    if age(-3) >= 1:
                        act.wait_ge(down_done, n)
                    relu(i, j - 3, 0)
                if has(0):
                    n, u, par = 2 * i + j, i + j // 2, j % 2
                    act.wait_ge(tmax_done, n + 1)
                    if age(0) >= 2:
                        act.wait_ge(max_in[par], 16 * u)
                    nc.scalar.copy(negmax_t[:, par, :], ps_max[1][0:HEADS, 0:TOK]).then_inc(maxt_done, 1)
                if has(2):
                    n, par = 2 * i + j + 2, j % 2
                    act.wait_ge(shift1_done, n + 1)
                    if age(2) >= 2:
                        act.wait_ge(tr1_done, n - 1)
                    for q in range(QT):
                        nc.scalar.activation(xn1[:, par, q, :],
                                             x_sb[:, bass.ds(n, 1), q, :].rearrange("p o d -> p (o d)"),
                                             ACT.Identity, scale=rstd1[:, par, q, :], bias=shift1[:, par, q, :]
                                             ).then_inc(xn1_done, 1)
                if has(-3):
                    relu(i, j - 3, 1)

            pipeline(act, step)

        @block.tensor
        def _(pe):
            ident = const("ident")
            pe.wait_ge(cst_in, 16)
            pe.wait_ge(ctx_in, 16)
            for c in range(2):
                nc.tensor.matmul(ps_max[c][:], const("wk_t"), ctx_sb[:, c * (B // 2):(c + 1) * (B // 2), 0:KEYS],
                                 start=True, stop=True).then_inc(k_proj, 1)

            def project_v():
                for n in range(B):
                    bank = ([ps_o] + ps_ring)[n // 4].rearrange("p a t -> p (a t)")
                    mm = nc.tensor.matmul(bank[:, (n % 4) * D:(n % 4 + 1) * D],
                                          ctx_sb[:, n, :], const("wv_t"), start=True, stop=True)
                    if n % 4 == 3:
                        mm.then_inc(v_proj, 1)
                pe.wait_ge(v_ready, 4)

            def scores_for_max(i, j, q, age):
                n, par = 2 * i + j, j % 2
                for half in range(2):
                    use = 2 * q + half
                    if age >= 1 or use >= 2:
                        pe.wait_ge(max_done, 4 * n + use - 1)
                    if age >= 1 and use == 1:
                        pe.wait_ge(maxt_done, n)
                    for g in (2 * half, 2 * half + 1):
                        mm = nc.tensor.matmul(ps_max[half][:, (g % 2) * GK:(g % 2 + 1) * GK],
                                              q_stack[0:SR, par, g, q * P:(q + 1) * P],
                                              k_diag[0:SR, par, g * GK:(g + 1) * GK], start=True, stop=True)
                    mm.then_inc(smax_done, 1)

            def scores_t(i, j, g, age, ffn_before):
                n, par = 2 * i + j, j % 2
                if g == 0 and age >= 1:
                    pe.wait_ge(exp_done, 4 * n)
                if g in (1, 2):
                    if ffn_before:
                        pe.wait_ge(hid_done, 4 * (n - 3) + 2 * g)
                    elif age >= 1:
                        pe.wait_ge(exp_done, 4 * (n - 1) + g + 1)
                if g == 3:
                    pe.wait_ge(exp_done, 4 * n + 1)
                for c in range(2):
                    mm = nc.tensor.matmul(ps_ring[(2 + g) % 3][:, c, :],
                                          k_diag[0:MR, par, (2 * g + c) * P:(2 * g + c + 1) * P],
                                          q_stack[0:MR, par, g, :], start=True, stop=True)
                mm.then_inc(s_done, 1)

            def up(i, j, half, exp_before):
                n, par = 2 * i + j, j % 2
                if exp_before:
                    pe.wait_ge(exp_done, 4 * (n + 2) + half + 2)
                for c in (2 * half, 2 * half + 1):
                    mm = nc.tensor.matmul(ps_ring[half][:, c % 2, :], w1_of(par, c), xn2_t[:, par, :],
                                          start=True, stop=True)
                mm.then_inc(up_done, 1)

            def down(i, j, half):
                n, par = 2 * i + j, j % 2
                pe.wait_ge(hid_done, 4 * n + 2 * half + 2)
                for c in (2 * half, 2 * half + 1):
                    for q in range(QT):
                        mm = nc.tensor.matmul(ps_pv[:, 0, q * P:(q + 1) * P], hid_t[:, c, q * P:(q + 1) * P],
                                              w2_of(par, c), start=(c == 0 and q == 0), stop=(c == FC - 1),
                                              skip_group_check=True)
                if half == 1:
                    mm.then_inc(down_done, 1)

            def heads_product(i, j, bank, part, weights, done):
                n = 2 * i + j
                for a in range(2):
                    pe.wait_ge(exp_done, GROUPS * n + 2 * a + 2)
                    for tile in range(4):
                        c = 4 * a + tile
                        mm = nc.tensor.matmul(bank[32 * tile:32 * (tile + 1), part, :], weights(a, c),
                                              probs_t[:, c, :], start=(a == 0), stop=(a == 1),
                                              tile_position=(0, 32 * tile))
                mm.then_inc(done, 1)

            def step(i, j, has, age):
                if has(0):
                    n, u, par = 2 * i + j, i + j // 2, j % 2
                    pe.wait_ge(qstack_in[par], 16 * GROUPS * (u + 1))
                    pe.wait_ge(kdiag_done, GROUPS * (n + 1))
                    scores_for_max(i, j, 0, age(0))
                if has(-1):
                    n, u, par = 2 * i + j - 1, i + (j - 1) // 2, (j - 1) % 2
                    pe.wait_ge(max_in[par], 16 * (u + 1))
                    scores_t(i, j - 1, 0, age(-1), has(-4))
                if has(1):
                    n = 2 * i + j + 1
                    pe.wait_ge(xn1t_done, n + 1)
                    nc.tensor.matmul(ps_q[:, 1, :], const("wq_t"), xn1_t[:], start=True, stop=True
                                     ).then_inc(q_proj, 1)
                if has(-4):
                    down(i, j - 4, 1)
                if has(-1):
                    for g in range(1, GROUPS):
                        scores_t(i, j - 1, g, age(-1), has(-4))
                if has(0):
                    scores_for_max(i, j, 1, age(0))
                if has(-2):
                    n, par = 2 * i + j - 2, (j - 2) % 2
                    pe.wait_ge(xn2_done, QT * (n + 1))
                    for q in range(QT):
                        mm = nc.tensor.transpose(ps_o[:, 1, q * P:(q + 1) * P], xn2[:, par, q, :], ident)
                    mm.then_inc(tr2_done, 1)
                if has(-3):
                    n, u, par = 2 * i + j - 3, i + (j - 3) // 2, (j - 3) % 2
                    pe.wait_ge(up_in[par], 16 * (u + 1))
                    up(i, j - 3, 0, has(-1))
                if has(-1):
                    n = 2 * i + j - 1
                    if has(1):
                        pe.wait_ge(q_done, n + 3)
                    elif has(-2):
                        pe.wait_ge(inv_done, n)
                    heads_product(i, j - 1, ps_q, 0,
                                  lambda a, c: cst[:, COL["v_mask"][0] + 32 * a:COL["v_mask"][0] + 32 * (a + 1)],
                                  sum_done)
                if has(0):
                    n, par = 2 * i + j, j % 2
                    pe.wait_ge(max_done, 4 * (n + 1))
                    for q in range(QT):
                        mm = nc.tensor.transpose(ps_max[1][0:HEADS, q * P:(q + 1) * P], negmax[:, par, q, :], ident)
                    mm.then_inc(tmax_done, 1)
                if has(-2):
                    n, par = 2 * i + j - 2, (j - 2) % 2
                    pe.wait_ge(xn2t_done, n + 1)
                    nc.tensor.matmul(ps_o[0:1, 0, 0:NE], tok_sum[:, par:par + 1], const("wr"),
                                     start=True, stop=True).then_inc(logit_done, 1)
                if has(-1):
                    n, par = 2 * i + j - 1, (j - 1) % 2
                    if has(-4):
                        pe.wait_ge(y_done, n - 2)
                    elif has(-2):
                        pe.wait_ge(attn_done, n)
                    pe.wait_ge(vdiag_done, n + 1)
                    heads_product(i, j - 1, ps_pv, 1, lambda a, c: v_diag[:, par, c, :], pv_done)
                if has(-3):
                    up(i, j - 3, 1, has(-1))
                if has(2):
                    n, par = 2 * i + j + 2, j % 2
                    pe.wait_ge(xn1_done, QT * (n + 1))
                    if has(-1):
                        pe.wait_ge(inv_done, n - 2)
                    elif has(1):
                        pe.wait_ge(q_done, n)
                    for q in range(QT):
                        mm = nc.tensor.transpose(ps_q[:, 0, q * P:(q + 1) * P], xn1[:, par, q, :], ident)
                    mm.then_inc(tr1_done, 1)
                if has(-1):
                    n = 2 * i + j - 1
                    pe.wait_ge(attn_done, n + 1)
                    if has(-2):
                        pe.wait_ge(route_done, n)
                    for q in range(QT):
                        mm = nc.tensor.matmul(ps_o[:, 0, q * P:(q + 1) * P], attn_t[:, q * P:(q + 1) * P],
                                              const("wo_t"), start=True, stop=True)
                    mm.then_inc(o_proj, 1)
                if has(-3):
                    n, u, par = 2 * i + j - 3, i + (j - 3) // 2, (j - 3) % 2
                    pe.wait_ge(down_in[par], 16 * (u + 1))
                    if has(-1):
                        pe.wait_ge(attn_done, n + 3)
                    elif age(-3) >= 1:
                        pe.wait_ge(y_done, n)
                    down(i, j - 3, 0)

            pipeline(pe, step, {-1: project_v})

        @block.vector
        def _(dve):
            dve.wait_ge(x_in[0], 16)
            dve.wait_ge(cst_in, 16)

            def prepare_k():
                a, b = COL["head_sel"]
                for par in range(2):
                    nc.vector.tensor_copy(
                        k_diag[SR:MR, par, :].rearrange("r (h k) -> r h k", h=HEADS),
                        cst[SR:MR, a:b].unsqueeze(2).to_broadcast([HEADS, HEADS, KEYS])).then_inc(sel_done, 1)
                for c in range(2):
                    cols = slice(c * 512, (c + 1) * 512)
                    dve.wait_ge(khi_done, c + 1)
                    nc.vector.scalar_tensor_tensor(
                        out=k_parts[:, 2, cols], in0=ps_max[c][:], scalar=const("bk_col"),
                        in1=k_parts[:, 0, cols].bitcast(F32), op0=ALU.add, op1=ALU.subtract).then_inc(khi_copied, 1)
                    nc.vector.tensor_copy(k_parts[:, 1, cols], k_parts[:, 0, cols].bitcast(F32)
                                          ).then_inc(khi_copied, 1)
                for k in range(1, len(x_in)):
                    dve.wait_ge(x_in[k], 16)

            def prepare_v():
                for c in range(4):
                    dve.wait_ge(v_proj, c + 1)
                    bank = ([ps_o] + ps_ring)[c]
                    nc.vector.tensor_tensor(v_sb[:, 4 * c:4 * (c + 1), :],
                                            bank.rearrange("p a (b d) -> p (a b) d", d=D),
                                            const("bv_row").unsqueeze(1).to_broadcast([P, 4, D]), ALU.add
                                            ).then_inc(v_ready, 1)
                dve.wait_ge(v_ready, 4)

            def reduce_max(i, j, q, half):
                n, par = 2 * i + j, j % 2
                dve.wait_ge(smax_done, 4 * n + 2 * q + half + 1)
                nc.vector.tensor_reduce(negmax[:, par, q, half * 8:(half + 1) * 8],
                                        ps_max[half][:].rearrange("p (h k) -> p h k", k=KEYS),
                                        AX_X, ALU.max, negate=True).then_inc(max_done, 1)

            def step(i, j, has, age):
                if has(0):
                    if age(0) >= 2:
                        dve.wait_ge(tmax_done, 2 * i + j - 1)
                    reduce_max(i, j, 0, 0)
                    reduce_max(i, j, 0, 1)
                if has(-2):
                    n, par = 2 * i + j - 2, (j - 2) % 2
                    dve.wait_ge(rstd2_done, n + 1)
                    if age(-2) >= 2:
                        dve.wait_ge(tr2_done, n - 1)
                    for q in range(QT):
                        nc.vector.tensor_scalar(xn2[:, par, q, :], x1[:, par, q, :], mv2[:, par, q, 0:1],
                                                rstd2[:, par, q, :], ALU.subtract, ALU.mult).then_inc(xn2_done, 1)
                if has(-4):
                    n, par = 2 * i + j - 4, (j - 4) % 2
                    dve.wait_ge(down_done, n + 1)
                    dve.wait_ge(x1b2_done, n + 1)
                    if age(-4) >= 1:
                        dve.wait_ge(y_out[1 - par], 16 * (i + (j - 5) // 2 + 1))
                    nc.vector.tensor_tensor(y_sb[:, par], ps_pv[:, 0, :].rearrange("p (q d) -> p q d", q=QT),
                                            x1_b2[:], ALU.add).then_inc(y_done, 1)
                if has(1):
                    n, u, par = 2 * i + j + 1, i + (j + 1) // 2, (j + 1) % 2
                    dve.wait_ge(qhi_done, n + 1)
                    if age(1) >= 2:
                        dve.wait_ge(qstack_in[par], 16 * GROUPS * u)
                    nc.vector.scalar_tensor_tensor(
                        out=q_parts[:, par, 1, :], in0=ps_q[:, 1, :], scalar=const("bq_col"),
                        in1=q_parts[:, par, 0, :].bitcast(F32), op0=ALU.add, op1=ALU.subtract
                    ).then_inc(q_done, 1)
                if has(2):
                    n, par = 2 * i + j + 2, j % 2
                    for q in range(QT):
                        st = nc.vector.bn_stats(stats1[:, par, q, :],
                                                x_sb[:, bass.ds(n, 1), q, :].rearrange("p o d -> p (o d)"))
                    st.then_inc(st1_raw, 1)
                    dve.wait_ge(st1_raw, n + 1)
                    if age(2) >= 2:
                        dve.wait_ge(shift1_done, n - 1)
                if has(0):
                    reduce_max(i, j, 1, 0)
                if has(2):
                    for q in range(QT):
                        st = nc.vector.bn_aggr(mv1[:, par, q, :], stats1[:, par, q, :])
                    st.then_inc(st1_done, 1)
                if has(0):
                    reduce_max(i, j, 1, 1)
                if has(-1):
                    n = 2 * i + j - 1
                    dve.wait_ge(sum_done, n + 1)
                    if age(-1) >= 1:
                        dve.wait_ge(attn_done, n)
                    nc.vector.reciprocal(inv_sum[:], ps_q[:, 0, :]).then_inc(inv_done, 1)
                    dve.wait_ge(inv_done, n + 1)
                    dve.wait_ge(pv_done, n + 1)
                    if age(-1) >= 1:
                        dve.wait_ge(o_proj, n)
                    nc.vector.tensor_tensor(attn_t[:], ps_pv[:, 1, :], inv_sum[:], ALU.mult).then_inc(attn_done, 1)
                if has(-2):
                    n, u, par = 2 * i + j - 2, i + (j - 2) // 2, (j - 2) % 2
                    dve.wait_ge(logit_done, n + 1)
                    if age(-2) >= 1:
                        dve.wait_ge(id_done, n)
                    if age(-2) >= 2:
                        dve.wait_ge(up_in[par], 16 * u)
                    nc.vector.scalar_tensor_tensor(out=route[:], in0=ps_o[0:1, 0, 0:NE], scalar=1.0 / TOK,
                                                   in1=const("br_row")[0:1], op0=ALU.mult, op1=ALU.add
                                                   ).then_inc(route_done, 1)
                    dve.wait_ge(route_done, n + 1)
                    hold(dve, i)
                    nc.vector.max(route_top[:], route[:]).then_inc(top_done, 1)
                    dve.wait_ge(top_done, n + 1)
                    hold(dve, i)
                    nc.vector.max_index(expert_id[:, par, :], route_top[:], route[:]).then_inc(id_done, 1)
                if has(-1):
                    n, par = 2 * i + j - 1, (j - 1) % 2
                    dve.wait_ge(o_proj, n + 1)
                    dve.wait_ge(xbo_done, n + 1)
                    if age(-1) >= 2:
                        dve.wait_ge(x1b2_done, n - 1)
                        dve.wait_ge(xn2_done, QT * (n - 1))
                    nc.vector.tensor_tensor(x1[:, par], ps_o[:, 0, :].rearrange("p (q d) -> p q d", q=QT),
                                            x_bo[:, par], ALU.add).then_inc(x1_done, 1)
                    dve.wait_ge(x1_done, n + 1)
                    for q in range(QT):
                        st = nc.vector.bn_stats(stats2[:, par, q, :], x1[:, par, q, :])
                    st.then_inc(st2_raw, 1)
                    dve.wait_ge(st2_raw, n + 1)
                    hold(dve, i)
                    for q in range(QT):
                        st = nc.vector.bn_aggr(mv2[:, par, q, :], stats2[:, par, q, :])
                    st.then_inc(st2_done, 1)

            pipeline(dve, step, {-2: prepare_k, -1: prepare_v})


_ARGS = ["x", "ctx_t", "consts", "experts"]


def kernel(**inputs):
    import concourse.bacc as _bacc
    from concourse.bass_utils import run_bass_kernel_spmd as _run

    a = {k: np.asarray(v) for k, v in inputs.items()}
    x, ctx = a["x"], a["ctx_1024"]
    B, TOK, D = x.shape
    KEYS = ctx.shape[1]
    W1, W2 = a["L0_ffn_W1"], a["L0_ffn_W2"]
    NE, _, F = W1.shape
    HD = D // HEADS
    f32 = np.float32

    order = np.arange(D).reshape(2, 4, 2, HD).transpose(1, 0, 2, 3).reshape(D)
    parts = {name: np.zeros((P, b - a_), f32) for name, (a_, b) in COL.items()}
    parts["ident"][:] = np.eye(P, dtype=f32)
    parts["wq_t"][:] = a["L0_xattn_Wq"].T
    parts["wk_t"][:] = a["L0_xattn_Wk"].T
    parts["wv_t"][:] = a["L0_xattn_Wv"].T[:, order]
    parts["wo_t"][:] = a["L0_xattn_Wo"].T[order]
    parts["bv_row"][:] = a["L0_xattn_bv"][order][None]
    parts["bo_row"][:] = a["L0_xattn_bo"][None]
    parts["wr"][:] = a["L0_ffn_Wr"]
    parts["br_row"][:] = a["L0_ffn_br"][None]
    parts["bq_col"][:, 0] = a["L0_xattn_bq"]
    parts["bk_col"][:, 0] = a["L0_xattn_bk"]
    rows = np.arange(PARTS * HG * HD)
    parts["k_mask"][rows, rows // (PARTS * HD)] = 1.0
    col = np.arange(64)
    parts["v_mask"][:] = ((col % 32) // 8)[None] == (2 * (col // 32))[None] + (np.arange(P) // KEYS)[:, None]
    parts["head_sel"][rows.size:rows.size + HEADS] = np.eye(HEADS, dtype=f32)
    consts = np.concatenate([parts[name] for name in COL], axis=1)
    experts = np.concatenate([
        W1,
        a["L0_ffn_b1"].reshape(NE, F // P, P).transpose(0, 2, 1),
        W2.reshape(NE, F // P, P, D).transpose(0, 2, 1, 3).reshape(NE, P, F // P * D),
        np.broadcast_to(a["L0_ffn_b2"][:, None, :], (NE, P, D)),
    ], axis=2)
    arrays = {"x": x, "ctx_t": np.concatenate([ctx, ctx], axis=1).transpose(0, 2, 1), "consts": consts, "experts": experts}

    nc = _bacc.Bacc("TRN2", target_bir_lowering=False, num_devices=1)
    in_map, args = {}, []
    for name in _ARGS:
        v = np.ascontiguousarray(arrays[name])
        in_map[f"in_{name}"] = v
        args.append(nc.dram_tensor(f"in_{name}", v.shape, mybir.dt.from_np(v.dtype), kind="ExternalInput").ap())
    args.append(nc.dram_tensor("out_y", x.shape, F32, kind="ExternalOutput").ap())
    xattn_moe_kernel(nc, *args)
    r = _run(nc, [in_map], core_ids=[0])
    return r.results[0]["out_y"]
```

```python
import numpy as np

import concourse.bass as bass
from concourse import mybir
from contextlib import ExitStack

F32 = mybir.dt.float32
F32R = mybir.dt.float32r
U32 = mybir.dt.uint32
ALU = mybir.AluOpType
ACT = mybir.ActivationFunctionType
AX_X = mybir.AxisListType.X

P = 128
HEADS = 16
HG = 4
GROUPS = HEADS // HG
PARTS = 3
EPS = 1e-5

_WIDTHS = [("ident", P), ("wq_t", P), ("wk_t", P), ("wr", 8), ("bq_col", 1), ("bk_col", 1), ("k_mask", HG),
           ("v_mask", 64), ("head_sel", HEADS), ("wv_t", P), ("wo_t", P), ("bv_row", P), ("bo_row", P), ("br_row", 8)]
COL = {}
_at = 0
for _name, _w in _WIDTHS:
    COL[_name] = (_at, _at + _w)
    _at += _w
CONST_W = _at
FIRST_W = COL["wv_t"][0]


def xattn_moe_kernel(nc, x, ctx_t, consts, experts, out):
    B, TOK, D = x.shape
    KEYS = ctx_t.shape[2] // 2
    QT = TOK // P
    HD = D // HEADS
    FC = 4
    F = FC * P
    NE = experts.shape[0]
    GR = HG * HD
    SR = PARTS * GR
    MR = SR + HEADS
    GK = HG * KEYS
    PAIRS = HEADS // 2
    SCALE = 1.0 / float(np.sqrt(np.float32(HD)))
    assert D == P and QT == 2 and 2 * KEYS == P and SR == 96

    with ExitStack() as ctx:
        def sb(name, shape, dt=F32):
            return ctx.enter_context(nc.sbuf_tensor(name, shape, dt))

        def psum(name, shape):
            return ctx.enter_context(nc.psum_tensor(name, shape, F32))

        def sem(name):
            return ctx.enter_context(nc.semaphore(name))

        cst = sb("cst", [P, CONST_W])
        ctx_sb = sb("ctx_sb", [P, B, 2 * KEYS])
        x_sb = sb("x_sb", [P, B, QT, D])
        minus_half = sb("minus_half", [P, QT])
        minus_one = sb("minus_one", [P, QT])
        eps_sb = sb("eps_sb", [P, QT])
        table_in = sb("table_in", [P, QT])
        stats1 = sb("stats1", [P, 2, QT, 6])
        mv1 = sb("mv1", [P, 2, QT, 2])
        rstd1 = sb("rstd1", [P, 2, QT, 1])
        ve1 = sb("ve1", [P, 2, QT, 1])
        nm1 = sb("nm1", [P, 2, QT, 1])
        shift1 = sb("shift1", [P, 2, QT, 1])
        stats2 = sb("stats2", [P, 2, QT, 6])
        mv2 = sb("mv2", [P, 2, QT, 2])
        rstd2 = sb("rstd2", [P, 2, QT, 1])
        ve2 = sb("ve2", [P, 2, QT, 1])
        xn1 = sb("xn1", [P, 2, QT, D])
        xn1_t = sb("xn1_t", [P, TOK])
        q_parts = sb("q_parts", [P, 2, PARTS, TOK], F32R)
        q_stack = sb("q_stack", [P, 2, GROUPS, TOK], F32R)
        k_parts = sb("k_parts", [P, PARTS, B * KEYS], F32R)
        k_stack = sb("k_stack", [SR, GROUPS, B * KEYS])
        k_diag = sb("k_diag", [P, 2, GROUPS * GK], F32R)
        v_sb = sb("v_sb", [P, B, D])
        v_diag = sb("v_diag", [P, 2, PAIRS, 32])
        negmax = sb("negmax", [P, 2, QT, HEADS])
        negmax_t = sb("negmax_t", [HEADS, 2, TOK], F32R)
        probs_t = sb("probs_t", [P, PAIRS, TOK])
        inv_sum = sb("inv_sum", [P, TOK])
        attn_t = sb("attn_t", [P, TOK])
        x_bo = sb("x_bo", [P, 2, QT, D])
        x1 = sb("x1", [P, 2, QT, D])
        x1_b2 = sb("x1_b2", [P, QT, D])
        xn2 = sb("xn2", [P, 2, QT, D])
        xn2_t = sb("xn2_t", [P, 2, TOK])
        tok_sum = sb("tok_sum", [P, 2])
        route = sb("route", [1, NE])
        route_top = sb("route_top", [1, 8])
        expert_id = sb("expert_id", [1, 2, 8], U32)
        EW = F + FC + F + D
        ew = sb("ew", [P, 2, EW])
        hid_t = sb("hid_t", [P, FC, TOK])
        y_sb = sb("y_sb", [P, 2, QT, D])

        ps_max = [psum(f"ps_max{k}", [P, 512]) for k in range(2)]
        ps_pv = psum("ps_pv", [P, 2, TOK])
        ps_q = psum("ps_q", [P, 2, TOK])
        ps_o = psum("ps_o", [P, 2, TOK])
        ps_ring = [psum(f"ps_ring{k}", [P, 2, TOK]) for k in range(3)]

        def const(name):
            a, b = COL[name]
            return cst[:, a:b]

        def b1_of(par, c):
            return ew[:, par, F + c:F + c + 1]

        def w2_of(par, c):
            return ew[:, par, F + FC + c * D:F + FC + (c + 1) * D]

        def b2_of(par):
            return ew[:, par, F + FC + F:EW]

        XLOADS = [0, 1, 4, 10, B]
        FIRST_B = B // 4
        KPIECES = [(0, FIRST_B, ps_max[0]), (FIRST_B, 3 * FIRST_B, ps_max[1]), (3 * FIRST_B, B,
                                                              ps_ring[0].rearrange("p a t -> p (a t)"))]
        V_BANKS = [ps_o, ps_pv, ps_ring[1], ps_ring[2]]
        x_in = [sem(f"x_in{k}") for k in range(len(XLOADS) - 1)]
        cst_in = [sem(f"cst_in{k}") for k in range(2)]
        ctx_in = [sem(f"ctx_in{k}") for k in range(2)]
        kstack_in = [sem(f"kstack_in{k}") for k in range(2)]
        qstack_in = [sem(f"qstack_in{k}") for k in range(2)]
        max_in = [sem(f"max_in{k}") for k in range(2)]
        up_in = [sem(f"up_in{k}") for k in range(2)]
        down_in = [sem(f"down_in{k}") for k in range(2)]
        y_out = [sem(f"y_out{k}") for k in range(2)]
        passed = [sem("sp_passed"), sem("dve_passed")]
        sel_done = sem("sel_done")
        khi_copied = sem("khi_copied")
        v_ready = sem("v_ready")
        st1_raw = sem("st1_raw")
        st1_done = sem("st1_done")
        max_done = sem("max_done")
        q_done = sem("q_done")
        inv_done = sem("inv_done")
        attn_done = sem("attn_done")
        x1_done = sem("x1_done")
        st2_raw = sem("st2_raw")
        st2_done = sem("st2_done")
        xn2_done = sem("xn2_done")
        route_done = sem("route_done")
        top_done = sem("top_done")
        id_done = sem("id_done")
        y_done = sem("y_done")
        khi_done = sem("khi_done")
        xn1_done = sem("xn1_done")
        xn1t_done = sem("xn1t_done")
        qhi_done = sem("qhi_done")
        qhi_copied = sem("qhi_copied")
        maxt_done = sem("maxt_done")
        hid_done = sem("hid_done")
        exp_done = sem("exp_done")
        xn2t_done = sem("xn2t_done")
        k_proj = sem("k_proj")
        v_proj = sem("v_proj")
        tr1_done = sem("tr1_done")
        q_proj = sem("q_proj")
        smax_done = sem("smax_done")
        tmax_done = sem("tmax_done")
        s_done = sem("s_done")
        sum_done = sem("sum_done")
        pv_done = sem("pv_done")
        o_proj = sem("o_proj")
        tr2_done = sem("tr2_done")
        logit_done = sem("logit_done")
        up_done = sem("up_done")
        down_done = sem("down_done")
        half_set = sem("half_set")
        ve1_done = sem("ve1_done")
        nm1_done = sem("nm1_done")
        rstd1_done = sem("rstd1_done")
        shift1_done = sem("shift1_done")
        vdiag_done = sem("vdiag_done")
        xbo_done = sem("xbo_done")
        kdiag_done = sem("kdiag_done")
        x1b2_done = sem("x1b2_done")
        ve2_done = sem("ve2_done")
        rstd2_done = sem("rstd2_done")

        LAST = B + 4

        def hold(engine, i):
            if not isinstance(i, int):
                engine.sem_inc(passed[engine is nc.vector], 1)

        def pipeline(engine, step, after_step=None):
            def peeled(t):
                step(0, t, lambda k: 0 <= t + k < B, lambda k: t + k)
                if after_step and t in after_step:
                    after_step[t]()
            for t in range(-3, 5):
                peeled(t)
            with engine.Fori(2, B // 2 - 2) as i:
                for j in (1, 2):
                    step(i, j, lambda k: True, lambda k: 4)
            for t in range(B - 3, LAST):
                peeled(t)

        block = ctx.enter_context(nc.Block())

        @block.sync
        def _(sp):
            def load_x(k):
                a, b = XLOADS[k], XLOADS[k + 1]
                sp.dma_start(x_sb[:, a:b], x[a:b].rearrange("b (p q) d -> p b q d", q=QT)).then_inc(x_in[k], 16)

            load_x(0)
            sp.dma_start(ctx_sb[:, 0:FIRST_B], ctx_t[0:FIRST_B].rearrange("b p k -> p b k")).then_inc(ctx_in[0], 16)
            load_x(1)
            load_x(2)
            load_x(3)

            def stack_k(b0, b1, pieces, landed):
                cols = slice(b0 * KEYS, b1 * KEYS)
                sp.wait_ge(khi_done, pieces)
                sp.wait_ge(khi_copied, 2 * pieces)
                for g in range(GROUPS):
                    sp.dma_start(k_stack[:, g, cols], k_parts[GR * g:GR * (g + 1), :, cols].bitcast(F32)
                                 ).then_inc(landed, 16)

            def step(i, j, has, age):
                if has(1):
                    n, u, par = 2 * i + j + 1, i + (j + 1) // 2, (j + 1) % 2
                    sp.wait_ge(q_done, n + 1)
                    sp.wait_ge(qhi_copied, n + 1)
                    hold(sp, i)
                    if age(1) >= 2:
                        sp.wait_ge(s_done, GROUPS * (n - 1))
                    for g in range(GROUPS):
                        sp.dma_start(q_stack[0:SR, par, g, :].bitcast(F32),
                                     q_parts[GR * g:GR * (g + 1), par].bitcast(F32)).then_inc(qstack_in[par], 16)
                if has(-4):
                    n, par = 2 * i + j - 4, (j - 4) % 2
                    sp.wait_ge(y_done, n + 1)
                    sp.dma_start(out[bass.ds(n, 1)].rearrange("b (p q) d -> p (b q d)", q=QT),
                                 y_sb[:, par].rearrange("p q d -> p (q d)")).then_inc(y_out[par], 16)
                if has(0):
                    n, par = 2 * i + j, j % 2
                    sp.wait_ge(maxt_done, n + 1)
                    sp.dma_start(q_stack[SR:MR, par].bitcast(F32),
                                 negmax_t[:, par, :].bitcast(F32).unsqueeze(1).to_broadcast([HEADS, GROUPS, TOK])
                                 ).then_inc(max_in[par], 16)
                if has(-2):
                    n, par = 2 * i + j - 2, (j - 2) % 2
                    sp.wait_ge(id_done, n + 1)
                    hold(sp, i)
                    if age(-2) >= 2:
                        sp.wait_ge(down_done, n - 1)
                        sp.wait_ge(x1b2_done, n - 1)
                        hold(sp, i)
                    e = sp.value_load(expert_id[0:1, par, 0:1], min_val=0, max_val=NE - 1)
                    for a, b, landed in ((0, F + FC, up_in), (F + FC, EW, down_in)):
                        sp.dma_start(ew[:, par, a:b], experts[bass.ds(e, 1), :, a:b].rearrange("o p c -> p (o c)")
                                     ).then_inc(landed[par], 16)

            pipeline(sp, step, {-2: lambda: stack_k(0, FIRST_B, 1, kstack_in[0]),
                                0: lambda: stack_k(FIRST_B, B, len(KPIECES), kstack_in[1])})
            for par in range(2):
                sp.wait_ge(y_out[par], 16 * (B // 2))

        @block.gpsimd
        def _(pool):
            nc.gpsimd.memset(minus_half[:], -0.5).then_inc(half_set, 1)
            nc.gpsimd.memset(eps_sb[:], EPS).then_inc(half_set, 1)
            nc.gpsimd.memset(minus_one[:], -1.0).then_inc(half_set, 1)

            def rsqrt(n, par, mv, ve, rstd, st_done, ve_done, rstd_done):
                pool.wait_ge(st_done, n + 1)
                nc.gpsimd.tensor_tensor(ve[:, par], mv[:, par, :, 1:2], eps_sb[:].unsqueeze(2), ALU.add
                                        ).then_inc(ve_done, 1)
                pool.wait_ge(ve_done, n + 1)
                nc.gpsimd.tensor_tensor(rstd[:, par], ve[:, par], minus_half[:].unsqueeze(2), ALU.pow
                                        ).then_inc(rstd_done, 1)

            def diag_k(i, j, age):
                n, par = 2 * i + j, j % 2
                if age == 0:
                    pool.wait_ge(kstack_in[0], 16 * GROUPS)
                if age >= 2:
                    pool.wait_ge(s_done, GROUPS * (n - 1))
                for g in range(GROUPS):
                    nc.gpsimd.tensor_tensor(
                        k_diag[0:SR, par, g * GK:(g + 1) * GK].rearrange("r (h k) -> r h k", h=HG),
                        k_stack[:, g, bass.ds(n * KEYS, KEYS)].unsqueeze(1).to_broadcast([SR, HG, KEYS]),
                        const("k_mask")[0:SR].unsqueeze(2).to_broadcast([SR, HG, KEYS]), ALU.mult
                    ).then_inc(kdiag_done, 1)

            def step(i, j, has, age):
                if has(-1):
                    n, par = 2 * i + j - 1, (j - 1) % 2
                    if age(-1) >= 2:
                        pool.wait_ge(x1_done, n - 1)
                    nc.gpsimd.tensor_tensor(x_bo[:, par], x_sb[:, bass.ds(n, 1)].rearrange("p o q d -> p (o q) d"),
                                            const("bo_row").unsqueeze(1).to_broadcast([P, QT, D]), ALU.add
                                            ).then_inc(xbo_done, 1)
                if has(-2):
                    rsqrt(2 * i + j - 2, (j - 2) % 2, mv2, ve2, rstd2, st2_done, ve2_done, rstd2_done)
                if has(1) and age(1) == 1:
                    diag_k(i, j + 1, 1)
                if has(2):
                    n, par = 2 * i + j + 2, j % 2
                    if age(2) >= 2:
                        pool.wait_ge(xn1_done, QT * (n - 1))
                    rsqrt(n, par, mv1, ve1, rstd1, st1_done, ve1_done, rstd1_done)
                    nc.gpsimd.tensor_tensor(nm1[:, par], mv1[:, par, :, 0:1], minus_one[:].unsqueeze(2), ALU.mult
                                            ).then_inc(nm1_done, 1)
                    pool.wait_ge(rstd1_done, n + 1)
                    pool.wait_ge(nm1_done, n + 1)
                    nc.gpsimd.tensor_tensor(shift1[:, par], nm1[:, par], rstd1[:, par], ALU.mult
                                            ).then_inc(shift1_done, 1)
                if has(-1):
                    n, par = 2 * i + j - 1, (j - 1) % 2
                    pool.wait_ge(v_ready, 4)
                    if age(-1) >= 2:
                        pool.wait_ge(pv_done, n - 1)
                    nc.gpsimd.tensor_tensor(
                        v_diag[:, par].rearrange("p (a t) c -> p a t c", a=2),
                        v_sb[:, bass.ds(n, 1), :].rearrange("p o (t c) -> p o t c", c=32).to_broadcast([P, 2, 4, 32]),
                        const("v_mask").rearrange("p (a c) -> p a c", a=2).unsqueeze(2).to_broadcast([P, 2, 4, 32]),
                        ALU.mult).then_inc(vdiag_done, 1)
                if has(-3):
                    n, u, par = 2 * i + j - 3, i + (j - 3) // 2, (j - 3) % 2
                    pool.wait_ge(down_in[par], 16 * (u + 1))
                    if age(-3) >= 1:
                        pool.wait_ge(y_done, n)
                    nc.gpsimd.tensor_tensor(x1_b2[:], x1[:, par],
                                            b2_of(par).unsqueeze(1).to_broadcast([P, QT, D]), ALU.add
                                            ).then_inc(x1b2_done, 1)
                if has(1) and age(1) != 1:
                    diag_k(i, j + 1, age(1))

            def constants_loaded():
                pool.wait_ge(cst_in[0], 16)
                pool.wait_ge(cst_in[1], 16)

            pool.wait_ge(half_set, 3)
            pipeline(pool, step, {-2: constants_loaded,
                                  FIRST_B - 2: lambda: pool.wait_ge(kstack_in[1], 16 * GROUPS)})

        @block.scalar
        def _(act):
            act.dma_start(cst[:, 0:FIRST_W], consts[:, 0:FIRST_W]).then_inc(cst_in[0], 16)
            act.dma_start(cst[:, FIRST_W:], consts[:, FIRST_W:]).then_inc(cst_in[1], 16)
            act.dma_start(ctx_sb[:, FIRST_B:], ctx_t[FIRST_B:].rearrange("b p k -> p b k")).then_inc(ctx_in[1], 16)
            act.wait_ge(half_set, 1)
            nc.scalar.activation(table_in[:], minus_half[:], ACT.Exp)

            def high_k(pieces):
                for c in pieces:
                    a, b, bank = KPIECES[c]
                    act.wait_ge(k_proj, c + 1)
                    nc.scalar.activation(k_parts[:, 0, a * KEYS:b * KEYS],
                                         bank[:, 0:(b - a) * KEYS], ACT.Identity,
                                         bias=const("bk_col")).then_inc(khi_done, 1)

            def exp_group(i, j, g):
                n = 2 * i + j
                act.wait_ge(s_done, GROUPS * n + g + 1)
                nc.scalar.activation(probs_t[:, 2 * g:2 * g + 2, :], ps_ring[(2 + g) % 3][:], ACT.Exp,
                                     scale=SCALE).then_inc(exp_done, 1)

            def relu(i, j, half):
                n, par = 2 * i + j, j % 2
                for c in (2 * half, 2 * half + 1):
                    act.wait_ge(up_done, 2 * n + half + 1)
                    nc.scalar.activation(hid_t[:, c, :], ps_ring[half][:, c % 2, :], ACT.Relu,
                                         bias=b1_of(par, c)).then_inc(hid_done, 1)

            def step(i, j, has, age):
                if has(-1):
                    if age(-1) >= 1:
                        act.wait_ge(pv_done, 2 * i + j - 1)
                    exp_group(i, j - 1, 0)
                if has(1):
                    n, u, par = 2 * i + j + 1, i + (j + 1) // 2, (j + 1) % 2
                    act.wait_ge(q_proj, n + 1)
                    if age(1) >= 2:
                        act.wait_ge(qstack_in[par], 16 * GROUPS * u)
                    nc.scalar.activation(q_parts[:, par, 0, :], ps_q[:, 1, :], ACT.Identity,
                                         bias=const("bq_col")).then_inc(qhi_done, 1)
                    act.wait_ge(qhi_done, n + 1)
                    nc.scalar.copy(q_parts[:, par, 2, :], q_parts[:, par, 0, :].bitcast(F32)).then_inc(qhi_copied, 1)
                if has(-1):
                    for g in range(1, GROUPS):
                        exp_group(i, j - 1, g)
                if has(-2):
                    n, par = 2 * i + j - 2, (j - 2) % 2
                    act.wait_ge(tr2_done, n + 1)
                    if age(-2) >= 2:
                        act.wait_ge(up_done, 2 * (n - 1))
                        act.wait_ge(logit_done, n - 1)
                    nc.scalar.activation(xn2_t[:, par, :], ps_o[:, 1, :], ACT.Identity,
                                         accum_out=tok_sum[:, par:par + 1]).then_inc(xn2t_done, 1)
                if has(0):
                    n, u, par = 2 * i + j, i + j // 2, j % 2
                    act.wait_ge(tmax_done, n + 1)
                    if age(0) >= 2:
                        act.wait_ge(max_in[par], 16 * u)
                    nc.scalar.copy(negmax_t[:, par, :], ps_max[1][0:HEADS, 0:TOK]).then_inc(maxt_done, 1)
                if has(2):
                    n, par = 2 * i + j + 2, j % 2
                    act.wait_ge(shift1_done, n + 1)
                    if age(2) >= 2:
                        act.wait_ge(tr1_done, n - 1)
                    for q in range(QT):
                        nc.scalar.activation(xn1[:, par, q, :],
                                             x_sb[:, bass.ds(n, 1), q, :].rearrange("p o d -> p (o d)"),
                                             ACT.Identity, scale=rstd1[:, par, q, :], bias=shift1[:, par, q, :]
                                             ).then_inc(xn1_done, 1)
                if has(1) and age(1) == 0:
                    high_k([1, 2])
                if has(2):
                    n = 2 * i + j + 2
                    act.wait_ge(tr1_done, n + 1)
                    if age(2) >= 1:
                        act.wait_ge(q_proj, n)
                    nc.scalar.copy(xn1_t[:], ps_q[:, 0, :]).then_inc(xn1t_done, 1)
                if has(-3):
                    act.wait_ge(up_in[(j - 3) % 2], 16 * (i + (j - 3) // 2 + 1))
                    if age(-3) >= 1:
                        act.wait_ge(down_done, 2 * i + j - 3)
                    relu(i, j - 3, 0)
                    relu(i, j - 3, 1)

            pipeline(act, step, {-2: lambda: high_k([0])})

        @block.tensor
        def _(pe):
            ident = const("ident")
            pe.wait_ge(cst_in[0], 16)

            def project_k(pieces):
                for c in pieces:
                    a, b, bank = KPIECES[c]
                    pe.wait_ge(ctx_in[min(c, 1)], 16)
                    nc.tensor.matmul(bank[:, 0:(b - a) * KEYS], const("wk_t"), ctx_sb[:, a:b, 0:KEYS],
                                     start=True, stop=True).then_inc(k_proj, 1)

            def project_v(quarters):
                pe.wait_ge(cst_in[1], 16)
                for n in range(4 * quarters[0], 4 * quarters[-1] + 4):
                    bank = V_BANKS[n // 4].rearrange("p a t -> p (a t)")
                    mm = nc.tensor.matmul(bank[:, (n % 4) * D:(n % 4 + 1) * D],
                                          ctx_sb[:, n, :], const("wv_t"), start=True, stop=True)
                    if n % 4 == 3:
                        mm.then_inc(v_proj, 1)

            def between(t):
                if t == -1:
                    project_k([1, 2])
                    project_v([0])
                if t == 0:
                    project_v([1])

            def banks_emptied():
                pe.wait_ge(v_ready, 4)

            def scores_for_max(i, j, q, age):
                n, par = 2 * i + j, j % 2
                for half in range(2):
                    use = 2 * q + half
                    if age >= 1 or use >= 2:
                        pe.wait_ge(max_done, 4 * n + use - 1)
                    if age >= 1 and use == 1:
                        pe.wait_ge(maxt_done, n)
                    for g in (2 * half, 2 * half + 1):
                        mm = nc.tensor.matmul(ps_max[half][:, (g % 2) * GK:(g % 2 + 1) * GK],
                                              q_stack[0:SR, par, g, q * P:(q + 1) * P],
                                              k_diag[0:SR, par, g * GK:(g + 1) * GK], start=True, stop=True)
                    mm.then_inc(smax_done, 1)

            def scores_t(i, j, g, age, ffn_before):
                n, par = 2 * i + j, j % 2
                if g == 0 and age >= 1:
                    pe.wait_ge(exp_done, 4 * n)
                if g in (1, 2):
                    if ffn_before:
                        pe.wait_ge(hid_done, 4 * (n - 3) + 2 * g)
                    elif age >= 1:
                        pe.wait_ge(exp_done, 4 * (n - 1) + g + 1)
                if g == 3:
                    pe.wait_ge(exp_done, 4 * n + 1)
                for c in range(2):
                    mm = nc.tensor.matmul(ps_ring[(2 + g) % 3][:, c, :],
                                          k_diag[0:MR, par, (2 * g + c) * P:(2 * g + c + 1) * P],
                                          q_stack[0:MR, par, g, :], start=True, stop=True)
                mm.then_inc(s_done, 1)

            def up(i, j, half, exp_before):
                n, par = 2 * i + j, j % 2
                if exp_before:
                    pe.wait_ge(exp_done, 4 * (n + 2) + half + 2)
                for c in (2 * half, 2 * half + 1):
                    mm = nc.tensor.matmul(ps_ring[half][:, c % 2, :], ew[:, par, c * P:(c + 1) * P],
                                          xn2_t[:, par, :], start=True, stop=True)
                mm.then_inc(up_done, 1)

            def down(i, j, half):
                n, par = 2 * i + j, j % 2
                pe.wait_ge(hid_done, 4 * n + 2 * half + 2)
                for c in (2 * half, 2 * half + 1):
                    for q in range(QT):
                        mm = nc.tensor.matmul(ps_pv[:, 0, q * P:(q + 1) * P], hid_t[:, c, q * P:(q + 1) * P],
                                              w2_of(par, c), start=(c == 0 and q == 0), stop=(c == FC - 1),
                                              skip_group_check=True)
                if half == 1:
                    mm.then_inc(down_done, 1)

            def heads_product(i, j, bank, part, weights, done):
                n = 2 * i + j
                for a in range(2):
                    pe.wait_ge(exp_done, GROUPS * n + 2 * a + 2)
                    for tile in range(4):
                        c = 4 * a + tile
                        mm = nc.tensor.matmul(bank[32 * tile:32 * (tile + 1), part, :], weights(a, c),
                                              probs_t[:, c, :], start=(a == 0), stop=(a == 1),
                                              tile_position=(0, 32 * tile))
                mm.then_inc(done, 1)

            def step(i, j, has, age):
                if has(0):
                    n, u, par = 2 * i + j, i + j // 2, j % 2
                    pe.wait_ge(qstack_in[par], 16 * GROUPS * (u + 1))
                    pe.wait_ge(kdiag_done, GROUPS * (n + 1))
                    if age(0) == 0:
                        pe.wait_ge(khi_copied, 2 * len(KPIECES))
                    scores_for_max(i, j, 0, age(0))
                if has(-1):
                    n, u, par = 2 * i + j - 1, i + (j - 1) // 2, (j - 1) % 2
                    pe.wait_ge(max_in[par], 16 * (u + 1))
                    scores_t(i, j - 1, 0, age(-1), has(-4))
                if has(1):
                    n = 2 * i + j + 1
                    pe.wait_ge(xn1t_done, n + 1)
                    nc.tensor.matmul(ps_q[:, 1, :], const("wq_t"), xn1_t[:], start=True, stop=True
                                     ).then_inc(q_proj, 1)
                if isinstance(i, int) and i == 0:
                    between(j)
                if has(-1):
                    for g in (1, 2):
                        scores_t(i, j - 1, g, age(-1), has(-4))
                if has(-4):
                    n, u, par = 2 * i + j - 4, i + (j - 4) // 2, (j - 4) % 2
                    pe.wait_ge(down_in[par], 16 * (u + 1))
                    if has(-2):
                        pe.wait_ge(attn_done, n + 3)
                    elif age(-4) >= 1:
                        pe.wait_ge(y_done, n)
                    down(i, j - 4, 0)
                if has(-1):
                    scores_t(i, j - 1, 3, age(-1), has(-4))
                if has(-4):
                    down(i, j - 4, 1)
                if has(0):
                    scores_for_max(i, j, 1, age(0))
                if has(-1):
                    n = 2 * i + j - 1
                    if has(1):
                        pe.wait_ge(q_done, n + 3)
                    elif has(-2):
                        pe.wait_ge(inv_done, n)
                    heads_product(i, j - 1, ps_q, 0,
                                  lambda a, c: cst[:, COL["v_mask"][0] + 32 * a:COL["v_mask"][0] + 32 * (a + 1)],
                                  sum_done)
                if has(-2):
                    n, par = 2 * i + j - 2, (j - 2) % 2
                    pe.wait_ge(xn2_done, QT * (n + 1))
                    for q in range(QT):
                        mm = nc.tensor.transpose(ps_o[:, 1, q * P:(q + 1) * P], xn2[:, par, q, :], ident)
                    mm.then_inc(tr2_done, 1)
                if has(0):
                    n, par = 2 * i + j, j % 2
                    pe.wait_ge(max_done, 4 * (n + 1))
                    for q in range(QT):
                        mm = nc.tensor.transpose(ps_max[1][0:HEADS, q * P:(q + 1) * P], negmax[:, par, q, :], ident)
                    mm.then_inc(tmax_done, 1)
                    if age(0) == 0:
                        project_v([2, 3])
                if has(-1):
                    n, par = 2 * i + j - 1, (j - 1) % 2
                    if has(-4):
                        pe.wait_ge(y_done, n - 2)
                    elif has(-2):
                        pe.wait_ge(attn_done, n)
                    pe.wait_ge(vdiag_done, n + 1)
                    heads_product(i, j - 1, ps_pv, 1, lambda a, c: v_diag[:, par, c, :], pv_done)
                if has(-2):
                    n, par = 2 * i + j - 2, (j - 2) % 2
                    pe.wait_ge(xn2t_done, n + 1)
                    nc.tensor.matmul(ps_o[0:1, 0, 0:NE], tok_sum[:, par:par + 1], const("wr"),
                                     start=True, stop=True).then_inc(logit_done, 1)
                if has(-3):
                    n = 2 * i + j - 3
                    pe.wait_ge(xn2t_done, n + 1)
                    pe.wait_ge(up_in[(j - 3) % 2], 16 * (i + (j - 3) // 2 + 1))
                    up(i, j - 3, 0, has(-1))
                if has(2):
                    n, par = 2 * i + j + 2, j % 2
                    pe.wait_ge(xn1_done, QT * (n + 1))
                    if has(-1):
                        pe.wait_ge(inv_done, n - 2)
                    elif has(1):
                        pe.wait_ge(q_done, n)
                    for q in range(QT):
                        mm = nc.tensor.transpose(ps_q[:, 0, q * P:(q + 1) * P], xn1[:, par, q, :], ident)
                    mm.then_inc(tr1_done, 1)
                if has(-3) and has(0):
                    up(i, j - 3, 1, has(-1))
                if has(-1):
                    n = 2 * i + j - 1
                    pe.wait_ge(attn_done, n + 1)
                    if has(-2):
                        pe.wait_ge(route_done, n)
                    for q in range(QT):
                        mm = nc.tensor.matmul(ps_o[:, 0, q * P:(q + 1) * P], attn_t[:, q * P:(q + 1) * P],
                                              const("wo_t"), start=True, stop=True)
                    mm.then_inc(o_proj, 1)
                if has(-3) and not has(0):
                    up(i, j - 3, 1, has(-1))

            pipeline(pe, step, {-2: lambda: project_k([0]), 0: banks_emptied})

        @block.vector
        def _(dve):
            dve.wait_ge(x_in[0], 16)

            def low_k(pieces):
                for c in pieces:
                    b0, b1, bank = KPIECES[c]
                    cols = slice(b0 * KEYS, b1 * KEYS)
                    dve.wait_ge(khi_done, c + 1)
                    nc.vector.scalar_tensor_tensor(
                        out=k_parts[:, 2, cols], in0=bank[:, 0:(b1 - b0) * KEYS], scalar=const("bk_col"),
                        in1=k_parts[:, 0, cols].bitcast(F32), op0=ALU.add, op1=ALU.subtract).then_inc(khi_copied, 1)
                    nc.vector.tensor_copy(k_parts[:, 1, cols], k_parts[:, 0, cols].bitcast(F32)
                                          ).then_inc(khi_copied, 1)

            def first_k():
                dve.wait_ge(cst_in[0], 16)
                dve.wait_ge(cst_in[1], 16)
                low_k([0])

            def rest():
                a, b = COL["head_sel"]
                for par in range(2):
                    nc.vector.tensor_copy(
                        k_diag[SR:MR, par, :].rearrange("r (h k) -> r h k", h=HEADS),
                        cst[SR:MR, a:b].unsqueeze(2).to_broadcast([HEADS, HEADS, KEYS])).then_inc(sel_done, 1)
                low_k([1, 2])
                v_of([0])

            def v_of(quarters):
                for c in quarters:
                    dve.wait_ge(v_proj, c + 1)
                    nc.vector.tensor_tensor(v_sb[:, 4 * c:4 * (c + 1), :],
                                            V_BANKS[c].rearrange("p a (b d) -> p (a b) d", d=D),
                                            const("bv_row").unsqueeze(1).to_broadcast([P, 4, D]), ALU.add
                                            ).then_inc(v_ready, 1)

            def later():
                v_of([1, 2, 3])
                dve.wait_ge(x_in[2], 16)

            def reduce_max(i, j, q, half):
                n, par = 2 * i + j, j % 2
                dve.wait_ge(smax_done, 4 * n + 2 * q + half + 1)
                nc.vector.tensor_reduce(negmax[:, par, q, half * 8:(half + 1) * 8],
                                        ps_max[half][:].rearrange("p (h k) -> p h k", k=KEYS),
                                        AX_X, ALU.max, negate=True).then_inc(max_done, 1)

            def step(i, j, has, age):
                if has(0):
                    if age(0) >= 2:
                        dve.wait_ge(tmax_done, 2 * i + j - 1)
                    reduce_max(i, j, 0, 0)
                if has(-2):
                    par = (j - 2) % 2
                    dve.wait_ge(st2_raw, 2 * i + j - 1)
                    hold(dve, i)
                    for q in range(QT):
                        st = nc.vector.bn_aggr(mv2[:, par, q, :], stats2[:, par, q, :])
                    st.then_inc(st2_done, 1)
                if has(0):
                    reduce_max(i, j, 0, 1)
                if has(1):
                    n, u, par = 2 * i + j + 1, i + (j + 1) // 2, (j + 1) % 2
                    dve.wait_ge(qhi_done, n + 1)
                    if age(1) >= 2:
                        dve.wait_ge(qstack_in[par], 16 * GROUPS * u)
                    nc.vector.scalar_tensor_tensor(
                        out=q_parts[:, par, 1, :], in0=ps_q[:, 1, :], scalar=const("bq_col"),
                        in1=q_parts[:, par, 0, :].bitcast(F32), op0=ALU.add, op1=ALU.subtract
                    ).then_inc(q_done, 1)
                if has(-2):
                    n, par = 2 * i + j - 2, (j - 2) % 2
                    dve.wait_ge(rstd2_done, n + 1)
                    if age(-2) >= 2:
                        dve.wait_ge(tr2_done, n - 1)
                    for q in range(QT):
                        nc.vector.tensor_scalar(xn2[:, par, q, :], x1[:, par, q, :], mv2[:, par, q, 0:1],
                                                rstd2[:, par, q, :], ALU.subtract, ALU.mult).then_inc(xn2_done, 1)
                if has(0):
                    reduce_max(i, j, 1, 0)
                    reduce_max(i, j, 1, 1)
                if has(-4):
                    n, par = 2 * i + j - 4, (j - 4) % 2
                    dve.wait_ge(down_done, n + 1)
                    dve.wait_ge(x1b2_done, n + 1)
                    if age(-4) >= 1:
                        dve.wait_ge(y_out[1 - par], 16 * (i + (j - 5) // 2 + 1))
                    nc.vector.tensor_tensor(y_sb[:, par], ps_pv[:, 0, :].rearrange("p (q d) -> p q d", q=QT),
                                            x1_b2[:], ALU.add).then_inc(y_done, 1)
                if has(-1):
                    n = 2 * i + j - 1
                    dve.wait_ge(sum_done, n + 1)
                    if age(-1) >= 1:
                        dve.wait_ge(attn_done, n)
                    nc.vector.reciprocal(inv_sum[:], ps_q[:, 0, :]).then_inc(inv_done, 1)
                if has(-2):
                    n, u, par = 2 * i + j - 2, i + (j - 2) // 2, (j - 2) % 2
                    dve.wait_ge(logit_done, n + 1)
                    if age(-2) >= 1:
                        dve.wait_ge(id_done, n)
                    if age(-2) >= 2:
                        dve.wait_ge(up_in[par], 16 * u)
                    nc.vector.scalar_tensor_tensor(out=route[:], in0=ps_o[0:1, 0, 0:NE], scalar=1.0 / TOK,
                                                   in1=const("br_row")[0:1], op0=ALU.mult, op1=ALU.add
                                                   ).then_inc(route_done, 1)
                if has(-1):
                    n = 2 * i + j - 1
                    dve.wait_ge(inv_done, n + 1)
                    dve.wait_ge(pv_done, n + 1)
                    if age(-1) >= 1:
                        dve.wait_ge(o_proj, n)
                    nc.vector.tensor_tensor(attn_t[:], ps_pv[:, 1, :], inv_sum[:], ALU.mult).then_inc(attn_done, 1)
                if has(3):
                    n, par = 2 * i + j + 3, (j + 3) % 2
                    if has(-2):
                        dve.wait_ge(route_done, n - 4)
                    for q in range(QT):
                        st = nc.vector.bn_stats(stats1[:, par, q, :],
                                                x_sb[:, bass.ds(n, 1), q, :].rearrange("p o d -> p (o d)"))
                    st.then_inc(st1_raw, 1)
                elif has(-2):
                    dve.wait_ge(route_done, 2 * i + j - 1)
                if has(-2):
                    nc.vector.max(route_top[:], route[:]).then_inc(top_done, 1)
                    dve.wait_ge(top_done, 2 * i + j - 1)
                if has(3):
                    dve.wait_ge(st1_raw, 2 * i + j + 4)
                    if age(3) >= 2:
                        dve.wait_ge(shift1_done, 2 * i + j + 2)
                if has(-1):
                    n, par = 2 * i + j - 1, (j - 1) % 2
                    dve.wait_ge(o_proj, n + 1)
                    dve.wait_ge(xbo_done, n + 1)
                    if age(-1) >= 2:
                        dve.wait_ge(x1b2_done, n - 1)
                    nc.vector.tensor_tensor(x1[:, par], ps_o[:, 0, :].rearrange("p (q d) -> p q d", q=QT),
                                            x_bo[:, par], ALU.add).then_inc(x1_done, 1)
                if has(-2):
                    nc.vector.max_index(expert_id[:, (j - 2) % 2, :], route_top[:], route[:]).then_inc(id_done, 1)
                if has(3):
                    par = (j + 3) % 2
                    for q in range(QT):
                        st = nc.vector.bn_aggr(mv1[:, par, q, :], stats1[:, par, q, :])
                    st.then_inc(st1_done, 1)
                if has(-1):
                    n, par = 2 * i + j - 1, (j - 1) % 2
                    dve.wait_ge(x1_done, n + 1)
                    for q in range(QT):
                        st = nc.vector.bn_stats(stats2[:, par, q, :], x1[:, par, q, :])
                    st.then_inc(st2_raw, 1)

            pipeline(dve, step, {-3: lambda: dve.wait_ge(x_in[1], 16), -2: first_k, -1: rest, 0: later,
                                 4: lambda: dve.wait_ge(x_in[3], 16)})


_ARGS = ["x", "ctx_t", "consts", "experts"]


def kernel(**inputs):
    import concourse.bacc as _bacc
    from concourse.bass_utils import run_bass_kernel_spmd as _run

    a = {k: np.asarray(v) for k, v in inputs.items()}
    x, ctx = a["x"], a["ctx_1024"]
    B, TOK, D = x.shape
    KEYS = ctx.shape[1]
    W1, W2 = a["L0_ffn_W1"], a["L0_ffn_W2"]
    NE, _, F = W1.shape
    HD = D // HEADS
    f32 = np.float32

    order = np.arange(D).reshape(2, 4, 2, HD).transpose(1, 0, 2, 3).reshape(D)
    parts = {name: np.zeros((P, b - a_), f32) for name, (a_, b) in COL.items()}
    parts["ident"][:] = np.eye(P, dtype=f32)
    parts["wq_t"][:] = a["L0_xattn_Wq"].T
    parts["wk_t"][:] = a["L0_xattn_Wk"].T
    parts["wv_t"][:] = a["L0_xattn_Wv"].T[:, order]
    parts["wo_t"][:] = a["L0_xattn_Wo"].T[order]
    parts["bv_row"][:] = a["L0_xattn_bv"][order][None]
    parts["bo_row"][:] = a["L0_xattn_bo"][None]
    parts["wr"][:] = a["L0_ffn_Wr"]
    parts["br_row"][:] = a["L0_ffn_br"][None]
    parts["bq_col"][:, 0] = a["L0_xattn_bq"]
    parts["bk_col"][:, 0] = a["L0_xattn_bk"]
    rows = np.arange(PARTS * HG * HD)
    parts["k_mask"][rows, rows // (PARTS * HD)] = 1.0
    col = np.arange(64)
    parts["v_mask"][:] = ((col % 32) // 8)[None] == (2 * (col // 32))[None] + (np.arange(P) // KEYS)[:, None]
    parts["head_sel"][rows.size:rows.size + HEADS] = np.eye(HEADS, dtype=f32)
    consts = np.concatenate([parts[name] for name in COL], axis=1)
    experts = np.concatenate([
        W1,
        a["L0_ffn_b1"].reshape(NE, F // P, P).transpose(0, 2, 1),
        W2.reshape(NE, F // P, P, D).transpose(0, 2, 1, 3).reshape(NE, P, F // P * D),
        np.broadcast_to(a["L0_ffn_b2"][:, None, :], (NE, P, D)),
    ], axis=2)
    arrays = {"x": x, "ctx_t": np.concatenate([ctx, ctx], axis=1).transpose(0, 2, 1), "consts": consts, "experts": experts}

    nc = _bacc.Bacc("TRN2", target_bir_lowering=False, num_devices=1)
    in_map, args = {}, []
    for name in _ARGS:
        v = np.ascontiguousarray(arrays[name])
        in_map[f"in_{name}"] = v
        args.append(nc.dram_tensor(f"in_{name}", v.shape, mybir.dt.from_np(v.dtype), kind="ExternalInput").ap())
    args.append(nc.dram_tensor("out_y", x.shape, F32, kind="ExternalOutput").ap())
    xattn_moe_kernel(nc, *args)
    r = _run(nc, [in_map], core_ids=[0])
    return r.results[0]["out_y"]
```
